# Optimizing a Trainium2 kernel written in Bass

```python
import numpy as np
import jax
import jax.numpy as jnp

def _softmax(x, axis=-1):
    return jax.nn.softmax(x, axis=axis)
def _gelu(x):
    return jax.nn.gelu(x, approximate=True)
def _silu(x):
    return jax.nn.silu(x)
def _sigmoid(x):
    return jax.nn.sigmoid(x)
def _layernorm(x, axis=-1, eps=1e-5):
    m = jnp.mean(x, axis=axis, keepdims=True)
    v = jnp.var(x, axis=axis, keepdims=True)
    return (x - m) / jnp.sqrt(v + eps)
def _scatter_add(tgt, idx, src, axis=0):
    return tgt.at[idx].add(src)
def _segment_sum(src, seg, n):
    return jax.ops.segment_sum(src, seg, n)

kernel_name = 'mk_conv_preact_d2_conv_nchw128_3c73a5'

def setup_inputs(seed: int = 0):
    np.random.seed(seed)
    _w = jnp.asarray
    def _rec_inputs():
        import jax
        import jax.numpy as jnp
        _gk = jax.random.key(seed)
        x = -7.109e-05 + 0.9999 * jax.random.normal(jax.random.fold_in(_gk, 1), (8, 128, 256, 256), jnp.float32)
        return x
    x = _rec_inputs()
    def _L0_conv_setup():
        import jax, jax.numpy as jnp
        import numpy as np
        B, C, H, W, O = (8, 128, 256, 256, 128)
        key = jax.random.key(seed)
        k1, k2, k3, k4 = jax.random.split(key, 4)
        x = jax.random.normal(k1, (B, C, H, W), dtype=jnp.float32)
        theta_s = jax.random.uniform(k2, (C, 2), dtype=jnp.float32, minval=-1.0, maxval=1.0)
        w_dw = jax.random.normal(k3, (C,), dtype=jnp.float32) * 0.1
        w_pw = jax.random.normal(k4, (O, C), dtype=jnp.float32) * (1.0 / np.sqrt(C))
        return {'x': x, 'theta_s': theta_s, 'w_dw': w_dw, 'w_pw': w_pw}
    _L0_conv_all = _L0_conv_setup()
    _L0_conv_in = {k: v for k, v in _L0_conv_all.items() if k in ('theta_s', 'w_dw', 'w_pw', )}
    del _L0_conv_all

    def _L1_conv_setup():
        import jax, jax.numpy as jnp
        import numpy as np
        from jax import lax
        EPS = 1e-05

        def haar_dwt(x):
            B, C, H, W = x.shape
            xr = x.reshape(B, C, H // 2, 2, W // 2, 2)
            x00 = xr[:, :, :, 0, :, 0]
            x01 = xr[:, :, :, 0, :, 1]
            x10 = xr[:, :, :, 1, :, 0]
            x11 = xr[:, :, :, 1, :, 1]
            ll = (x00 + x01 + x10 + x11) * 0.5
            lh = (x00 + x01 - x10 - x11) * 0.5
            hl = (x00 - x01 + x10 - x11) * 0.5
            hh = (x00 - x01 - x10 + x11) * 0.5
            return (ll, lh, hl, hh)

        def haar_idwt(ll, lh, hl, hh):
            y00 = (ll + lh + hl + hh) * 0.5
            y01 = (ll + lh - hl - hh) * 0.5
            y10 = (ll - lh + hl - hh) * 0.5
            y11 = (ll - lh - hl + hh) * 0.5
            B, C, H, W = ll.shape
            top = jnp.stack([y00, y01], axis=-1)
            bot = jnp.stack([y10, y11], axis=-1)
            y = jnp.stack([top, bot], axis=3)
            return y.reshape(B, C, 2 * H, 2 * W)

        def conv1x1(x, w, b):
            return jnp.einsum('bchw,oc->bohw', x, w) + b[None, :, None, None]

        def batchnorm(x, g, b):
            mu = jnp.mean(x, axis=(0, 2, 3), keepdims=True)
            var = jnp.var(x, axis=(0, 2, 3), keepdims=True)
            xh = (x - mu) * lax.rsqrt(var + EPS)
            return xh * g[None, :, None, None] + b[None, :, None, None]

        def layernorm_chw(x, g, b):
            mu = jnp.mean(x, axis=(1, 2, 3), keepdims=True)
            var = jnp.var(x, axis=(1, 2, 3), keepdims=True)
            xh = (x - mu) * lax.rsqrt(var + EPS)
            return xh * g[None, :, None, None] + b[None, :, None, None]

        def dwconv3x3(x, w, b):
            C = x.shape[1]
            y = lax.conv_general_dilated(x, w, (1, 1), [(1, 1), (1, 1)], dimension_numbers=('NCHW', 'OIHW', 'NCHW'), feature_group_count=C)
            return y + b[None, :, None, None]
        gelu = lambda x: jax.nn.gelu(x, approximate=False)
        key = jax.random.key(seed)
        ks = jax.random.split(key, 16)
        C = 128
        B, H, W = (8, 256, 256)
        f = jnp.float32
        s = lambda k, shape, fan: jax.random.normal(k, shape, f) * (1.0 / np.sqrt(fan))
        return {'x': jax.random.normal(ks[0], (B, C, H, W), f), 'w_c1': s(ks[1], (C, 4 * C), 4 * C), 'b_c1': jnp.zeros((C,), f), 'bn1_g': jnp.ones((C,), f), 'bn1_b': jnp.zeros((C,), f), 'dw_w': s(ks[2], (C, 1, 3, 3), 9), 'dw_b': jnp.zeros((C,), f), 'gn_g': jnp.ones((C,), f), 'gn_b': jnp.zeros((C,), f), 'pw1_w': s(ks[3], (C, C), C), 'pw1_b': jnp.zeros((C,), f), 'pw2_w': s(ks[4], (C, C), C), 'pw2_b': jnp.zeros((C,), f), 'w_c2': s(ks[5], (4 * C, C), C), 'b_c2': jnp.zeros((4 * C,), f), 'bn2_g': jnp.ones((4 * C,), f), 'bn2_b': jnp.zeros((4 * C,), f)}
    _L1_conv_all = _L1_conv_setup()
    _L1_conv_in = {k: v for k, v in _L1_conv_all.items() if k in ('w_c1', 'b_c1', 'bn1_g', 'bn1_b', 'dw_w', 'dw_b', 'gn_g', 'gn_b', 'pw1_w', 'pw1_b', 'pw2_w', 'pw2_b', 'w_c2', 'b_c2', 'bn2_g', 'bn2_b', )}
    del _L1_conv_all

    return {
        "x": x,
        "L0_conv_theta_s": _L0_conv_in["theta_s"],
        "L0_conv_w_dw": _L0_conv_in["w_dw"],
        "L0_conv_w_pw": _L0_conv_in["w_pw"],
        "L1_conv_w_c1": _L1_conv_in["w_c1"],
        "L1_conv_b_c1": _L1_conv_in["b_c1"],
        "L1_conv_bn1_g": _L1_conv_in["bn1_g"],
        "L1_conv_bn1_b": _L1_conv_in["bn1_b"],
        "L1_conv_dw_w": _L1_conv_in["dw_w"],
        "L1_conv_dw_b": _L1_conv_in["dw_b"],
        "L1_conv_gn_g": _L1_conv_in["gn_g"],
        "L1_conv_gn_b": _L1_conv_in["gn_b"],
        "L1_conv_pw1_w": _L1_conv_in["pw1_w"],
        "L1_conv_pw1_b": _L1_conv_in["pw1_b"],
        "L1_conv_pw2_w": _L1_conv_in["pw2_w"],
        "L1_conv_pw2_b": _L1_conv_in["pw2_b"],
        "L1_conv_w_c2": _L1_conv_in["w_c2"],
        "L1_conv_b_c2": _L1_conv_in["b_c2"],
        "L1_conv_bn2_g": _L1_conv_in["bn2_g"],
        "L1_conv_bn2_b": _L1_conv_in["bn2_b"],
    }

def reference(x, L0_conv_theta_s, L0_conv_w_dw, L0_conv_w_pw, L1_conv_w_c1, L1_conv_b_c1, L1_conv_bn1_g, L1_conv_bn1_b, L1_conv_dw_w, L1_conv_dw_b, L1_conv_gn_g, L1_conv_gn_b, L1_conv_pw1_w, L1_conv_pw1_b, L1_conv_pw2_w, L1_conv_pw2_b, L1_conv_w_c2, L1_conv_b_c2, L1_conv_bn2_g, L1_conv_bn2_b):
    import jax
    import jax.numpy as jnp
    def _L0_conv_ref(x, theta_s, w_dw, w_pw):
        import jax, jax.numpy as jnp
        import numpy as np
        B, C, H, W, O = (8, 128, 256, 256, 128)
        b, c, h, w = x.shape
        xp = jnp.pad(x, ((0, 0), (0, 0), (1, 1), (1, 1)))
        hp, wp = (h + 2, w + 2)
        t = -theta_s
        ft = jnp.floor(t)
        dt = t - ft
        ft = ft.astype(jnp.int32)
        m = jnp.arange(1, h + 1)
        n = jnp.arange(1, w + 1)
        y0 = jnp.clip(m[None, :] + ft[:, 0:1], 0, hp - 1)
        y1 = jnp.clip(m[None, :] + ft[:, 0:1] + 1, 0, hp - 1)
        x0 = jnp.clip(n[None, :] + ft[:, 1:2], 0, wp - 1)
        x1 = jnp.clip(n[None, :] + ft[:, 1:2] + 1, 0, wp - 1)
        cidx = jnp.arange(c)[:, None, None]
        z1 = xp[:, cidx, y0[:, :, None], x0[:, None, :]]
        z2 = xp[:, cidx, y0[:, :, None], x1[:, None, :]]
        z3 = xp[:, cidx, y1[:, :, None], x0[:, None, :]]
        z4 = xp[:, cidx, y1[:, :, None], x1[:, None, :]]
        dy = dt[:, 0][None, :, None, None]
        dx = dt[:, 1][None, :, None, None]
        s = z1 * (1 - dy) * (1 - dx) + z2 * (1 - dy) * dx + z3 * dy * (1 - dx) + z4 * dy * dx
        s = s * w_dw[None, :, None, None]
        return jnp.einsum('bchw,oc->bohw', s, w_pw)

    def _L1_conv_ref(x, w_c1, b_c1, bn1_g, bn1_b, dw_w, dw_b, gn_g, gn_b, pw1_w, pw1_b, pw2_w, pw2_b, w_c2, b_c2, bn2_g, bn2_b):
        import jax, jax.numpy as jnp
        import numpy as np
        from jax import lax
        EPS = 1e-05

        def haar_dwt(x):
            B, C, H, W = x.shape
            xr = x.reshape(B, C, H // 2, 2, W // 2, 2)
            x00 = xr[:, :, :, 0, :, 0]
            x01 = xr[:, :, :, 0, :, 1]
            x10 = xr[:, :, :, 1, :, 0]
            x11 = xr[:, :, :, 1, :, 1]
            ll = (x00 + x01 + x10 + x11) * 0.5
            lh = (x00 + x01 - x10 - x11) * 0.5
            hl = (x00 - x01 + x10 - x11) * 0.5
            hh = (x00 - x01 - x10 + x11) * 0.5
            return (ll, lh, hl, hh)

        def haar_idwt(ll, lh, hl, hh):
            y00 = (ll + lh + hl + hh) * 0.5
            y01 = (ll + lh - hl - hh) * 0.5
            y10 = (ll - lh + hl - hh) * 0.5
            y11 = (ll - lh - hl + hh) * 0.5
            B, C, H, W = ll.shape
            top = jnp.stack([y00, y01], axis=-1)
            bot = jnp.stack([y10, y11], axis=-1)
            y = jnp.stack([top, bot], axis=3)
            return y.reshape(B, C, 2 * H, 2 * W)

        def conv1x1(x, w, b):
            return jnp.einsum('bchw,oc->bohw', x, w) + b[None, :, None, None]

        def batchnorm(x, g, b):
            mu = jnp.mean(x, axis=(0, 2, 3), keepdims=True)
            var = jnp.var(x, axis=(0, 2, 3), keepdims=True)
            xh = (x - mu) * lax.rsqrt(var + EPS)
            return xh * g[None, :, None, None] + b[None, :, None, None]

        def layernorm_chw(x, g, b):
            mu = jnp.mean(x, axis=(1, 2, 3), keepdims=True)
            var = jnp.var(x, axis=(1, 2, 3), keepdims=True)
            xh = (x - mu) * lax.rsqrt(var + EPS)
            return xh * g[None, :, None, None] + b[None, :, None, None]

        def dwconv3x3(x, w, b):
            C = x.shape[1]
            y = lax.conv_general_dilated(x, w, (1, 1), [(1, 1), (1, 1)], dimension_numbers=('NCHW', 'OIHW', 'NCHW'), feature_group_count=C)
            return y + b[None, :, None, None]
        gelu = lambda x: jax.nn.gelu(x, approximate=False)
        ll, lh, hl, hh = haar_dwt(x)
        h = jnp.concatenate([ll, lh, hl, hh], axis=1)
        h = gelu(batchnorm(conv1x1(h, w_c1, b_c1), bn1_g, bn1_b))
        res = h
        o = dwconv3x3(h, dw_w, dw_b)
        o = layernorm_chw(o, gn_g, gn_b)
        o = conv1x1(o, pw1_w, pw1_b)
        o = gelu(o)
        o = conv1x1(o, pw2_w, pw2_b)
        h = o + res
        h = gelu(batchnorm(conv1x1(h, w_c2, b_c2), bn2_g, bn2_b))
        C = h.shape[1] // 4
        return haar_idwt(h[:, :C], h[:, C:2 * C], h[:, 2 * C:3 * C], h[:, 3 * C:])

    def _gn(v, G=32, eps=1e-5):
        B_, C_, H_, W_ = v.shape
        g = v.reshape(B_, G, C_ // G, H_, W_)
        m = jnp.mean(g, axis=(2, 3, 4), keepdims=True)
        s = jnp.var(g, axis=(2, 3, 4), keepdims=True)
        return ((g - m) / jnp.sqrt(s + eps)).reshape(v.shape)

    def _ln_c(v, eps=1e-6):
        m = jnp.mean(v, axis=1, keepdims=True)
        s = jnp.var(v, axis=1, keepdims=True)
        return (v - m) / jnp.sqrt(s + eps)

    def _ln_t(v, eps=1e-5):
        m = jnp.mean(v, axis=-1, keepdims=True)
        s = jnp.var(v, axis=-1, keepdims=True)
        return (v - m) / jnp.sqrt(s + eps)

    def _to_tokens(v):
        B_, C_, H_, W_ = v.shape
        return v.reshape(B_, C_, H_ * W_).transpose(0, 2, 1)
    def _from_tokens(t, like):
        B_, C_, H_, W_ = like.shape
        return t.transpose(0, 2, 1).reshape(B_, C_, H_, W_)

    x = x + _L0_conv_ref(_gn(x), L0_conv_theta_s, L0_conv_w_dw, L0_conv_w_pw)
    x = x + _L1_conv_ref(_gn(x), L1_conv_w_c1, L1_conv_b_c1, L1_conv_bn1_g, L1_conv_bn1_b, L1_conv_dw_w, L1_conv_dw_b, L1_conv_gn_g, L1_conv_gn_b, L1_conv_pw1_w, L1_conv_pw1_b, L1_conv_pw2_w, L1_conv_pw2_b, L1_conv_w_c2, L1_conv_b_c2, L1_conv_bn2_g, L1_conv_bn2_b)
    return x


_drawn_inputs = setup_inputs


def setup_inputs(seed=0):
    import zlib

    import numpy as np

    out = dict(_drawn_inputs(seed))
    spreads = {'L1_conv_b_c1': (0.0, 0.8),
     'L1_conv_bn1_g': (1.0, 0.2),
     'L1_conv_bn1_b': (0.0, 0.1),
     'L1_conv_dw_b': (0.0, 0.1),
     'L1_conv_gn_g': (1.0, 0.2),
     'L1_conv_gn_b': (0.0, 0.302),
     'L1_conv_pw1_b': (0.0, 0.1),
     'L1_conv_pw2_b': (0.0, 0.8),
     'L1_conv_b_c2': (0.0, 0.8),
     'L1_conv_bn2_g': (1.0, 0.2),
     'L1_conv_bn2_b': (0.0, 0.1)}
    factors = {}
    for name, (base, spread) in spreads.items():
        noise = np.random.default_rng([zlib.crc32(name.encode()), seed]).standard_normal(out[name].shape)
        drawn = base * np.exp(spread * noise) if base else spread * noise
        out[name] = jnp.asarray(drawn.astype(out[name].dtype))
    for name, factor in factors.items():
        out[name] = (out[name] * factor).astype(out[name].dtype)
    return out
```

```python
from contextlib import ExitStack

import concourse.bass as bass
from concourse import mybir

F32 = mybir.dt.float32
BF16 = mybir.dt.bfloat16
ALU = mybir.AluOpType
ACT = mybir.ActivationFunctionType

P = 128
B, H, W = 8, 256, 256
HH, HW = H // 2, W // 2
G = 4
BANK = 512
ROWS = 8
CH = ROWS * W
NCH = H // ROWS
SLOTS = 4
NG = NCH // SLOTS
HC = CH // 4
TROWS = 8
TILE = TROWS * HW
NT = HH // TROWS
PE_TAPS = [(0, 0), (0, 1), (0, 2), (1, 0)]
DVE_TAPS = [(1, 1), (1, 2), (2, 0), (2, 1), (2, 2)]
EPS = 1e-5
TINY = 2.0 ** -30
LEAD = 4

assert HC == BANK and NCH % SLOTS == 0 and TILE == 2 * BANK


def preact_kernel(nc, x, theta_s, w_dw, w_pwT, w_c1T, b_c1, bn1_g, bn1_b, dw_w, dw_b, gn_g, gn_b,
                  pw1_wT, pw1_b, pw2_wT, pw2_b, w_c2T, b_c2, bn2_g, bn2_b, out):
    x1_dram = nc.dram_tensor("x1_dram", (B * NCH, P, CH), F32, kind="Internal").ap()
    y1_dram = nc.dram_tensor("y1_dram", (B * NT, P, TILE), F32, kind="Internal").ap()
    h2_dram = nc.dram_tensor("h2_dram", (B * NT, P, TILE), F32, kind="Internal").ap()

    with ExitStack() as ctx:
        def sb(name, shape, dt=F32):
            return ctx.enter_context(nc.sbuf_tensor(name, shape, dt))

        def sem(name):
            return ctx.enter_context(nc.semaphore(name))

        ident = sb("ident", [P, P])
        group_mean = sb("group_mean", [P, P])
        all_mean = sb("all_mean", [P, P])
        ones = sb("ones", [P, W])
        theta = sb("theta", [P, 2])
        wdw = sb("wdw", [P, 1])
        pwT = sb("pwT", [P, P])
        c1T = sb("c1T", [P, 4, P])
        c1H = sb("c1H", [P, 4, P])
        bc1 = sb("bc1", [P, 1])
        bn1 = sb("bn1", [P, 2])
        taps = sb("taps", [P, 9])
        tap_diag = sb("tap_diag", [P, len(PE_TAPS), P])
        bdw = sb("bdw", [P, 1])
        gn = sb("gn", [P, 2])
        pw1T = sb("pw1T", [P, P])
        bpw1 = sb("bpw1", [P, 1])
        pw2T = sb("pw2T", [P, P])
        bpw2 = sb("bpw2", [P, 1])
        c2T = sb("c2T", [P, 4, P])
        bc2 = sb("bc2", [P, 4])
        bn2 = sb("bn2", [P, 2, 4])

        shift = sb("shift", [P, 8])
        center_y, center_x = shift[:, 0:1], shift[:, 1:2]
        up, left = shift[:, 2:3], shift[:, 3:4]
        down, right = shift[:, 4:5], shift[:, 5:6]
        center_w, inv_center_y = shift[:, 6:7], shift[:, 7:8]

        small = sb("small", [P, 40])
        mom = small[:, 0:2]
        gmom = small[:, 2:4]
        var, std, rstd, tmp = (small[:, k:k + 1] for k in range(4, 8))
        scale0, scale0r, q0, bias0 = (small[:, k:k + 1] for k in range(8, 12))
        pad_u = small[:, 12:13]
        q1, bias1, h_scale, h_bias = (small[:, k:k + 1] for k in range(13, 17))
        ln_scale, ln_shift, bias_pw1, h2_mean = (small[:, k:k + 1] for k in range(17, 21))
        z_mean, z_scale, z_bias = small[:, 21:25], small[:, 25:29], small[:, 29:33]
        z_tmp, z_std = small[:, 33:37], sb("z_std", [P, 4])
        h2_mean_row = sb("h2_mean_row", [1, 2, P])

        w_center = sb("w_center", [P, P])
        w_right = sb("w_right", [P, P])
        w_c1b = sb("w_c1b", [P, 4, P])
        w_pw1b = sb("w_pw1b", [P, P])
        stats_x = sb("stats_x", [P, NCH * 4 * 6])
        sums_x1 = sb("sums_x1", [P, 2, NCH])
        stats_y1 = sb("stats_y1", [P, B * NCH * 6])
        stats_o = sb("stats_o", [P, NT * 2 * 6])
        gram = sb("gram", [P, P + 1])
        cov_w = sb("cov_w", [P, 4, P])

        arena = sb("arena", [P, 38500])
        at = [0]

        def cut(n):
            at[0] += n
            assert at[0] <= 38500
            return arena[:, at[0] - n:at[0]]

        ring = cut((SLOTS * ROWS + 2) * W).rearrange("p (r c) -> p r c", c=W)
        u_buf = [cut(ROWS * (W + 2)).rearrange("p (r c) -> p r c", c=W + 2) for _ in range(2)]
        v_buf = [cut(CH) for _ in range(2)]
        x1_buf = [cut(CH) for _ in range(2)]
        squares = cut(CH // 2).bitcast(BF16)
        y1_out = [cut(TILE) for _ in range(2)]
        at[0] = 0
        h_pad = cut((HH + 2) * (HW + 2)).rearrange("p (r c) -> p r c", c=HW + 2)
        o_all = cut(HH * HW).rearrange("p (r c) -> p r c", c=HW)
        y1_in = o_in = [cut(TILE) for _ in range(2)]
        a_buf = [cut(BANK) for _ in range(2)]
        h2_buf = [cut(BANK) for _ in range(2)]
        hT_buf = [cut(4 * (P + 1)).rearrange("p (k c) -> p k c", k=4) for _ in range(2)]
        at[0] = (SLOTS * ROWS + 2) * W
        h2_in = [cut(TILE) for _ in range(2)]
        g_buf = [cut(4 * HC).rearrange("p (q n) -> p q n", q=4) for _ in range(2)]
        s_buf = [cut(4 * HC).rearrange("p (q n) -> p q n", q=4) for _ in range(2)]

        ps = ctx.enter_context(nc.psum_tensor("ps", [P, 8, BANK], F32))
        ps_small = ps[:, 7, :]

        def slot(s, above=0, below=0):
            return ring[:, 1 + s * ROWS - above:1 + (s + 1) * ROWS + below, :]

        params_in = sem("params_in")
        passed = sem("passed")
        consts_made = sem("consts_made")
        setup_done = sem("setup_done")
        dve_step = sem("dve_step")
        mom_ready, gmom_ready = sem("mom_ready"), sem("gmom_ready")
        var_ready, std_ready = sem("var_ready"), sem("std_ready")
        vec_ready, vec_done = sem("vec_ready"), sem("vec_done")
        shift_ready, c1_ready = sem("shift_ready"), sem("c1_ready")
        bn1_ready, ln_ready, bn2_ready = sem("bn1_ready"), sem("ln_ready"), sem("bn2_ready")
        cov_ready, cov_done = sem("cov_ready"), sem("cov_done")
        slot_in = [sem(f"slot_in{s}") for s in range(SLOTS)]
        u_up, u_done, v_done = sem("u_up"), sem("u_done"), sem("v_done")
        dw_acc, dw_counted = sem("dw_acc"), sem("dw_counted")
        halves_done, out_ready = sem("halves_done"), sem("out_ready")
        y1_loaded = [sem(f"y1_loaded{k}") for k in range(2)]
        h2_loaded = [sem(f"h2_loaded{k}") for k in range(2)]
        xe_loaded = [sem(f"xe_loaded{s}") for s in range(SLOTS)]
        x_counted, conv_done, x1_ready, sq_done = sem("x_counted"), sem("conv_done"), sem("x1_ready"), sem("sq_done")
        c1_done, y1_ready, y1_counted = sem("c1_done"), sem("y1_ready"), sem("y1_counted")
        h_ready, dw_done, dw_taken = sem("h_ready"), sem("dw_done"), sem("dw_taken")
        pw1_done, a_ready, pw2_done, h2_ready = sem("pw1_done"), sem("a_ready"), sem("pw2_done"), sem("h2_ready")
        hT_done, hT_ready = sem("hT_done"), sem("hT_ready")
        gram_done, gram_added = sem("gram_done"), sem("gram_added")
        c2_done, g_ready, s_done = sem("c2_done"), sem("g_ready"), sem("s_done")
        x1_stored = [sem(f"x1_stored{k}") for k in range(2)]
        y1_stored = [sem(f"y1_stored{k}") for k in range(2)]
        h2_stored = [sem(f"h2_stored{k}") for k in range(2)]
        out_stored = [sem(f"out_stored{s}") for s in range(SLOTS)]

        def nth(t, back=0):
            return t + (1 + LEAD - back)

        CONSTS = 7
        PARAMS = [(theta[:, :], theta_s), (wdw[:, :], w_dw), (pwT[:, :], w_pwT), (c1T[:, :, :], w_c1T),
                  (bc1[:, :], b_c1), (bn1[:, 0:1], bn1_g), (bn1[:, 1:2], bn1_b), (taps[:, :], dw_w),
                  (bdw[:, :], dw_b), (gn[:, 0:1], gn_g), (gn[:, 1:2], gn_b), (pw1T[:, :], pw1_wT),
                  (bpw1[:, :], pw1_b), (pw2T[:, :], pw2_wT), (bpw2[:, :], pw2_b), (c2T[:, :, :], w_c2T),
                  (bc2[:, :], b_c2), (bn2[:, 0, :], bn2_g), (bn2[:, 1, :], bn2_b)]

        def wait_alone(eng, value, *sems):
            for s_ in sems:
                eng.wait_ge(s_, value)
            eng.sem_inc(passed, 1)

        block = ctx.enter_context(nc.Block())

        @block.sync
        def _(sp):
            for dst, src in PARAMS:
                sp.dma_start(dst, src).then_inc(params_in, 16)

            def load_x(b, g, s, above=0, below=0):
                sp.dma_start(slot(s, above, below),
                             x[b, :, bass.ds(((g * SLOTS + s) * ROWS - above) * W, (ROWS + above + below) * W)]
                             .rearrange("p (r c) -> p r c", c=W)).then_inc(slot_in[s], 16)

            def load_shift_group(b, g, first=False, last=False):
                for s in range(SLOTS):
                    if first:
                        sp.wait_ge(x_counted, nth(b * NCH + (NCH - SLOTS + s)))
                    else:
                        sp.wait_ge(x1_ready, nth(b * NCH + g * SLOTS + s, SLOTS))
                    load_x(b, g, s, int(s == 0 and not first), int(s == SLOTS - 1 and not last))

            with sp.Fori(0, B) as b:
                wait_alone(sp, nth(b * NCH, 1), c1_done)
                with sp.Fori(0, NG) as g:
                    for s in range(SLOTS):
                        sp.wait_ge(x_counted, nth(b * NCH + g * SLOTS + s, SLOTS))
                        load_x(b, g, s)
                load_shift_group(b, 0, first=True)
                with sp.Fori(1, NG - 1) as g:
                    load_shift_group(b, g)
                load_shift_group(b, NG - 1, last=True)
                sp.wait_ge(x1_ready, nth(b * NCH, 1 - NCH))
                wait_alone(sp, b * (16 * NCH // 2) + (16 * NCH // 2 + 16), *x1_stored)
                with sp.Fori(0, NG) as g:
                    for s in range(SLOTS):
                        sp.wait_ge(c1_done, nth(b * NCH + g * SLOTS + s, SLOTS))
                        sp.dma_start(slot(s), x1_dram[b * NCH + g * SLOTS + s]
                                     .rearrange("p (r c) -> p r c", c=W)).then_inc(slot_in[s], 16)

            for k in range(2):
                sp.wait_ge(y1_stored[k], 16 * (B * NT // 2) + 16)
            sp.wait_ge(bn1_ready, 1)
            with sp.Fori(0, B) as b:
                with sp.Fori(0, NT // 2) as i:
                    for k in range(2):
                        sp.wait_ge(h_ready, nth(b * NT + i * 2 + k, 2))
                        sp.dma_start(y1_in[k], y1_dram[b * NT + i * 2 + k]).then_inc(y1_loaded[k], 16)
                with sp.Fori(0, NT) as j:
                    for k in range(2):
                        sp.wait_ge(h2_ready, nth(b * (2 * NT) + j * 2 + k))
                        sp.dma_start(h2_dram[b * NT + j, :, k * BANK:(k + 1) * BANK], h2_buf[k]
                                     ).then_inc(h2_stored[k], 16)

            for k in range(2):
                sp.wait_ge(h2_stored[k], 16 * (B * NT) + 16)
            sp.wait_ge(bn2_ready, 1)

            def load_output_group(g):
                for s in range(SLOTS):
                    if s % 2 == 0:
                        sp.wait_ge(c2_done, nth(g * SLOTS + s, SLOTS - 1))
                        sp.dma_start(h2_in[s // 2], h2_dram[g * 2 + s // 2]).then_inc(h2_loaded[s // 2], 16)
                    if not isinstance(g, int):
                        sp.wait_ge(out_stored[s], g * 16)
                    sp.dma_start(slot(s), x1_dram[g * SLOTS + s].rearrange("p (r c) -> p r c", c=W)
                                 ).then_inc(xe_loaded[s], 16)

            load_output_group(0)
            with sp.Fori(1, B * NG) as g:
                load_output_group(g)
            for s in range(SLOTS):
                sp.wait_ge(out_stored[s], 16 * (B * NG))

        @block.gpsimd
        def _(pool):
            pool.memset(ident[:, :], 0.0).then_inc(consts_made, 1)
            pool.memset(group_mean[:, :], 1.0 / G).then_inc(consts_made, 1)
            pool.memset(all_mean[:, :], 1.0 / P).then_inc(consts_made, 1)
            pool.memset(ones[:, :], 1.0).then_inc(consts_made, 1)
            pool.wait_ge(consts_made, 4)
            pool.affine_select(out=ident[:, :], in_=ident[:, :], compare_op=ALU.not_equal, fill=1.0, base=0,
                               pattern=[[-1, P]], channel_multiplier=1).then_inc(consts_made, 1)
            groups = group_mean[:, :].rearrange("p (g c) -> p g c", c=G)
            pool.affine_select(out=groups, in_=groups, compare_op=ALU.is_ge, fill=0.0, base=0,
                               pattern=[[-G, P // G], [0, G]], channel_multiplier=1).then_inc(consts_made, 1)
            pool.wait_ge(consts_made, 6)
            pool.affine_select(out=groups, in_=groups, compare_op=ALU.is_ge, fill=0.0, base=G - 1,
                               pattern=[[G, P // G], [0, G]], channel_multiplier=-1).then_inc(consts_made, 1)
            with pool.Fori(0, B) as b:
                with pool.Fori(0, NG) as g:
                    for s in range(SLOTS):
                        pool.wait_ge(out_ready, b * NCH + g * SLOTS + (s + 1))
                        pool.dma_start(out[b, :, bass.ds((g * SLOTS + s) * CH, CH)]
                                       .rearrange("p (r c) -> p r c", c=W), slot(s)).then_inc(out_stored[s], 16)

        @block.scalar
        def _(act):
            for stored in x1_stored + y1_stored + h2_stored:
                act.sem_inc(stored, 16)
            for counter in (sq_done, y1_ready, h_ready, a_ready, hT_ready, g_ready):
                act.sem_inc(counter, LEAD)

            def square_root(n):
                act.wait_ge(var_ready, n)
                nc.scalar.activation(std, var, ACT.Sqrt).then_inc(std_ready, 1)

            def square_group(b, g):
                for s in range(SLOTS):
                    i = g * SLOTS + s
                    act.wait_ge(x1_ready, nth(b * NCH + i))
                    act.dma_start(x1_dram[b * NCH + i], x1_buf[s % 2]).then_inc(x1_stored[s % 2], 16)
                    act.wait_ge(sq_done, nth(b * NCH + i, 1))
                    nc.scalar.activation(squares, x1_buf[s % 2], ACT.Square,
                                         accum_out=sums_x1[:, 1, bass.ds(i, 1)]).then_inc(sq_done, 1)

            def y1_group(b, g):
                for s in range(SLOTS):
                    t = b * NCH + g * SLOTS + s
                    k = s // 2
                    act.wait_ge(c1_done, nth(t))
                    if s % 2 == 0:
                        act.wait_ge(y1_stored[k], b * (16 * NG) + g * 16 + 16)
                        act.wait_ge(y1_counted, nth(t, SLOTS - 1))
                    nc.scalar.activation(y1_out[k][:, (s % 2) * HC:(s % 2 + 1) * HC], ps[:, s, :],
                                         ACT.Identity, bias=bias1).then_inc(y1_ready, 1)
                    if s % 2 == 1:
                        act.wait_ge(y1_ready, nth(t))
                        act.dma_start(y1_dram[b * NT + g * 2 + k], y1_out[k]).then_inc(y1_stored[k], 16)

            with act.Fori(0, B) as b:
                square_root(b * 2 + 1)
                with act.Fori(0, NG) as g:
                    square_group(b, g)
                square_root(b * 2 + 2)
                act.wait_ge(c1_ready, b + 1)
                with act.Fori(0, NG) as g:
                    y1_group(b, g)
            square_root(2 * B + 1)

            act.wait_ge(bn1_ready, 1)
            with act.Fori(0, B) as b:
                act.wait_ge(h2_ready, nth(b * (2 * NT), 1))
                with act.Fori(0, NT // 2) as i:
                    for k in range(2):
                        act.wait_ge(y1_loaded[k], b * (16 * NT // 2) + i * 16 + 16)
                        nc.scalar.activation(h_pad[:, bass.ds((i * 2 + k) * TROWS + 1, TROWS), 1:HW + 1],
                                             y1_in[k].rearrange("p (r c) -> p r c", c=HW), ACT.Gelu,
                                             bias=h_bias, scale=h_scale).then_inc(h_ready, 1)
                square_root(b + (2 * B + 2))
                act.wait_ge(ln_ready, b + 1)
                with act.Fori(0, NT) as j:
                    n = b * (2 * NT) + j * 2
                    for k in range(2):
                        act.wait_ge(pw1_done, nth(n + k))
                        act.wait_ge(pw2_done, nth(n + k, 2))
                        nc.scalar.activation(a_buf[k], ps[:, k, :], ACT.Gelu, bias=bias_pw1).then_inc(a_ready, 1)
                    for k in range(2):
                        act.wait_ge(hT_done, nth(n + k))
                        act.wait_ge(gram_done, nth(b * NT + j, 1))
                        nc.scalar.activation(hT_buf[k][:, :, 0:P], ps[:, 4 + k, :].rearrange("p (k c) -> p k c", k=4),
                                             ACT.Copy).then_inc(hT_ready, 1)

            act.wait_ge(var_ready, 3 * B + 2)
            nc.scalar.activation(z_std[:, :], z_tmp, ACT.Sqrt).then_inc(std_ready, 1)
            act.wait_ge(bn2_ready, 1)
            with act.Fori(0, B * NCH // 2) as i:
                for k in range(2):
                    act.wait_ge(c2_done, nth(i * 2 + k))
                    act.wait_ge(s_done, nth(i * 2 + k, 2))
                    for q in range(4):
                        last = nc.scalar.activation(g_buf[k][:, q, :], ps[:, 4 * k + q, :], ACT.Gelu,
                                                    bias=z_bias[:, q:q + 1], scale=z_scale[:, q:q + 1])
                    last.then_inc(g_ready, 1)

        @block.tensor
        def _(pe):
            mm = nc.tensor.matmul
            for counter in (conv_done, c1_done, dw_done, pw1_done, pw2_done, hT_done, gram_done, c2_done):
                pe.sem_inc(counter, LEAD)

            def channel_means(n, weights):
                pe.wait_ge(mom_ready, n)
                mm(ps_small[:, 0:2], weights[:, :], mom, start=True, stop=True).then_inc(gmom_ready, 1)

            def vector_product(n, weights, vec):
                pe.wait_ge(vec_ready, n)
                mm(ps_small[:, 4:5], weights, vec, start=True, stop=True).then_inc(vec_done, 1)

            def shift_group(b, g):
                for s in range(SLOTS):
                    t = b * NCH + g * SLOTS + s
                    k = s % 2
                    pe.wait_ge(v_done, t + 1)
                    pe.wait_ge(x1_ready, nth(t, 2))
                    for r in range(4):
                        mm(ps[:, 4 * k + r, :], w_center[:, :], v_buf[k][:, r * BANK:(r + 1) * BANK],
                           start=True, stop=False)
                        last = mm(ps[:, 4 * k + r, :], w_right[:, :], u_buf[k][:, 2 * r:2 * r + 2, 2:W + 2],
                                  start=False, stop=True)
                    last.then_inc(conv_done, 1)

            def c1_group(b, g):
                for s in range(SLOTS):
                    t = b * NCH + g * SLOTS + s
                    pe.wait_ge(slot_in[s], b * (48 * NG) + g * 16 + (32 * NG + 16))
                    pe.wait_ge(y1_ready, nth(t, SLOTS))
                    cells = slot(s).rearrange("p (r a) (c e) -> p a e r c", a=2, e=2)
                    for q in range(4):
                        last = mm(ps[:, s, :], w_c1b[:, q, :], cells[:, q // 2, q % 2, :, :],
                                  start=(q == 0), stop=(q == 3))
                    last.then_inc(c1_done, 1)

            pe.wait_ge(setup_done, 1)
            with pe.Fori(0, B) as b:
                channel_means(b * 2 + 1, group_mean)
                vector_product(b * 2 + 1, pwT[:, :], q0)
                wait_alone(pe, b + 1, shift_ready)
                with pe.Fori(0, NG) as g:
                    shift_group(b, g)
                channel_means(b * 2 + 2, group_mean)
                vector_product(b * 2 + 2, c1T[:, 0, :], q1)
                wait_alone(pe, b + 1, c1_ready)
                with pe.Fori(0, NG) as g:
                    c1_group(b, g)

            def dw_tile(b, j, last_tile=False):
                pe.wait_ge(h_ready, nth(b * NT + j, 0 if last_tile else -1))
                for k in range(2):
                    pe.wait_ge(dw_taken, nth(b * (2 * NT) + j * 2 + k, 2))
                    for n, (dy, dx) in enumerate(PE_TAPS):
                        last = mm(ps[:, 6 + k, :], tap_diag[:, n, :],
                                  h_pad[:, bass.ds(j * TROWS + (4 * k + dy), 4), dx:dx + HW],
                                  start=(n == 0), stop=(n == len(PE_TAPS) - 1))
                    last.then_inc(dw_done, 1)

            pe.wait_ge(bn1_ready, 1)
            with pe.Fori(0, B) as b:
                wait_alone(pe, nth(b * NT, 1), gram_added)
                with pe.Fori(0, NT - 1) as j:
                    dw_tile(b, j)
                dw_tile(b, NT - 1, last_tile=True)
                channel_means(b + (2 * B + 1), all_mean)
                vector_product(b + (2 * B + 1), pw1T[:, :], ln_shift)
                wait_alone(pe, b + 1, ln_ready)
                with pe.Fori(0, NT) as j:
                    n = b * (2 * NT) + j * 2
                    for k in range(2):
                        pe.wait_ge(a_ready, nth(n + k, 2))
                        mm(ps[:, k, :], w_pw1b[:, :], o_all[:, bass.ds(j * TROWS + 4 * k, 4), :],
                           start=True, stop=True).then_inc(pw1_done, 1)
                    for k in range(2):
                        pe.wait_ge(a_ready, nth(n + k))
                        pe.wait_ge(h2_ready, nth(n + k, 2))
                        mm(ps[:, 2 + k, :], pw2T[:, :], a_buf[k], start=True, stop=True).then_inc(pw2_done, 1)
                    for k in range(2):
                        pe.wait_ge(h2_ready, nth(n + k))
                        pe.wait_ge(hT_ready, nth(n + k, 2))
                        for c in range(4):
                            last = nc.tensor.transpose(ps[:, 4 + k, c * P:(c + 1) * P],
                                                       h2_buf[k][:, c * P:(c + 1) * P], ident[:, :])
                        last.then_inc(hT_done, 1)
                    pe.wait_ge(gram_added, nth(b * NT + j, 1))
                    for k in range(2):
                        pe.wait_ge(hT_ready, nth(n + k))
                        for c in range(4):
                            last = mm(ps[:, 6, 0:P + 1], hT_buf[k][:, c, 0:P], hT_buf[k][:, c, :],
                                      start=(k == 0 and c == 0), stop=(k == 1 and c == 3))
                    last.then_inc(gram_done, 1)

            pe.wait_ge(cov_ready, 1)
            mm(ps[0:1, 0, 0:P], h2_mean, ident[:, :], start=True, stop=True).then_inc(cov_done, 1)
            pe.wait_ge(cov_ready, 2)
            mm(ps[:, 1, 0:P], h2_mean_row[:, 0, :], h2_mean_row[:, 1, :], start=True, stop=True).then_inc(cov_done, 1)
            pe.wait_ge(cov_ready, 3)
            mm(ps[:, 2, :], gram[:, 0:P], c2T[:, :, :], start=True, stop=True)
            for q in range(4):
                last = mm(ps[:, 3, q:q + 1], c2T[:, q, :], h2_mean, start=True, stop=True)
            last.then_inc(cov_done, 1)
            pe.wait_ge(cov_ready, 4)
            for q in range(4):
                last = mm(ps[:, 4, q:q + 1], cov_w[:, q, :], ones[:, 0:1], start=True, stop=True)
            last.then_inc(cov_done, 1)

            pe.wait_ge(bn2_ready, 1)
            with pe.Fori(0, B * NG) as g:
                for s in range(SLOTS):
                    k = s % 2
                    if k == 0:
                        pe.wait_ge(h2_loaded[s // 2], g * 16 + 16)
                    pe.wait_ge(g_ready, nth(g * SLOTS + s, 2))
                    for q in range(4):
                        last = mm(ps[:, 4 * k + q, :], c2T[:, q, :], h2_in[s // 2][:, k * HC:(k + 1) * HC],
                                  start=True, stop=True)
                    last.then_inc(c2_done, 1)

        @block.vector
        def _(dve):
            stt, ts, tt = nc.vector.scalar_tensor_tensor, nc.vector.tensor_scalar, nc.vector.tensor_tensor
            for counter in (x_counted, x1_ready, y1_counted, dw_taken, h2_ready, gram_added, s_done):
                dve.sem_inc(counter, LEAD)

            steps = [0, 0]

            def start_steps(base):
                steps[0], steps[1] = base, 0

            def done(ins):
                steps[1] += 1
                ins.then_inc(dve_step, 1)
                dve.wait_ge(dve_step, steps[0] + steps[1])

            def refine(r, s, v):
                done(nc.vector.reciprocal(r, s))
                done(tt(s, r, r, ALU.mult))
                done(tt(s, s, v, ALU.mult))
                done(ts(s, s, -0.5, 1.5, ALU.mult, ALU.add))
                done(tt(r, r, s, ALU.mult))

            def normaliser(n, nth_root):
                dve.wait_ge(gmom_ready, n)
                done(nc.vector.tensor_copy(gmom, ps_small[:, 0:2]))
                done(stt(out=tmp, in0=gmom[:, 0:1], scalar=gmom[:, 0:1], in1=gmom[:, 1:2],
                         op0=ALU.mult, op1=ALU.subtract))
                done(ts(tmp, tmp, 0.0, -1.0, ALU.min, ALU.mult))
                root(nth_root)

            def root(n):
                ts(var, tmp, EPS, None, ALU.add).then_inc(var_ready, 1)
                dve.wait_ge(std_ready, n)
                refine(rstd, std, var)

            dve.wait_ge(params_in, 16 * len(PARAMS))
            dve.wait_ge(consts_made, CONSTS)
            start_steps(0)
            for axis, center, inverse, before, after in ((0, center_y, inv_center_y, up, down),
                                                         (1, center_x, center_w, left, right)):
                th = theta[:, axis:axis + 1]
                done(ts(tmp, th, -1.0, None, ALU.mult))
                done(tt(center, th, tmp, ALU.max))
                done(ts(center, center, -1.0, 1.0, ALU.mult, ALU.add))
                done(ts(center, center, TINY, None, ALU.max))
                done(nc.vector.reciprocal(inverse, center))
                done(ts(before, th, 0.0, None, ALU.max))
                done(tt(before, before, inverse, ALU.mult))
                done(ts(after, tmp, 0.0, None, ALU.max))
                done(tt(after, after, inverse, ALU.mult))
            done(tt(center_w, center_y, center_x, ALU.mult))
            done(tt(center_w, center_w, wdw[:, :], ALU.mult))
            ll, lh, hl, hh = (c1T[:, q, :] for q in range(4))
            tt(cov_w[:, 0, :], ll, lh, ALU.add)
            tt(cov_w[:, 1, :], ll, lh, ALU.subtract)
            tt(cov_w[:, 2, :], hl, hh, ALU.add)
            done(tt(cov_w[:, 3, :], hl, hh, ALU.subtract))
            tt(c1H[:, 0, :], cov_w[:, 0, :], cov_w[:, 2, :], ALU.add)
            tt(c1H[:, 1, :], cov_w[:, 0, :], cov_w[:, 2, :], ALU.subtract)
            tt(c1H[:, 2, :], cov_w[:, 1, :], cov_w[:, 3, :], ALU.add)
            done(tt(c1H[:, 3, :], cov_w[:, 1, :], cov_w[:, 3, :], ALU.subtract))
            done(ts(c1H[:, :, :], c1H[:, :, :], 0.5, None, ALU.mult))
            for n, (dy, dx) in enumerate(PE_TAPS):
                ts(tap_diag[:, n, :], ident[:, :], taps[:, 3 * dy + dx:3 * dy + dx + 1], None, ALU.mult)
            nc.vector.memset(gram[:, :], 0.0).then_inc(setup_done, 1)
            dve.wait_ge(setup_done, 1)
            SETUP_STEPS = 23
            assert steps[1] == SETUP_STEPS

            def count_x_group(b, g):
                for s in range(SLOTS):
                    dve.wait_ge(slot_in[s], b * (48 * NG) + g * 16 + 16)
                    rows = slot(s).rearrange("p r c -> p (r c)")
                    for r in range(4):
                        last = nc.vector.bn_stats(stats_x[:, bass.ds((g * SLOTS + s) * 24 + 6 * r, 6)],
                                                  rows[:, r * BANK:(r + 1) * BANK])
                    last.then_inc(x_counted, 1)

            def shift_rows(b, g, s, last_group=False):
                t = b * NCH + g * SLOTS + s
                k = s % 2
                for near in range(s, min(s + 2, SLOTS)):
                    dve.wait_ge(slot_in[near], b * (48 * NG) + g * 16 + (16 * NG + 16))
                dve.wait_ge(conv_done, nth(t, 2))
                u = u_buf[k][:, :, 1:W + 1]
                stt(out=u, in0=ring[:, s * ROWS:(s + 1) * ROWS, :], scalar=up, in1=slot(s),
                    op0=ALU.mult, op1=ALU.add).then_inc(u_up, 1)
                dve.wait_ge(u_up, t + 1)
                stt(out=u, in0=ring[:, s * ROWS + 2:(s + 1) * ROWS + 2, :], scalar=down, in1=u,
                    op0=ALU.mult, op1=ALU.add).then_inc(u_done, 1)
                dve.wait_ge(u_done, t + 1)
                stt(out=v_buf[k].rearrange("p (r c) -> p r c", c=W), in0=u_buf[k][:, :, 0:W], scalar=left, in1=u,
                    op0=ALU.mult, op1=ALU.add).then_inc(v_done, 1)

            def make_x1(b, g, s):
                i = g * SLOTS + s
                t = b * NCH + i
                k = s % 2
                dve.wait_ge(conv_done, nth(t))
                dve.wait_ge(x1_stored[k], b * (8 * NCH) + g * (8 * SLOTS) + (s // 2 * 16 + 16))
                dve.wait_ge(sq_done, nth(t, 2))
                stt(out=x1_buf[k], in0=ps[:, 4 * k:4 * k + 4, :].rearrange("p a n -> p (a n)"), scalar=bias0,
                    in1=slot(s).rearrange("p r c -> p (r c)"), op0=ALU.add, op1=ALU.add,
                    accum_out=sums_x1[:, 0, bass.ds(i, 1)]).then_inc(x1_ready, 1)

            def shift_group(b, g, first=False):
                for s in range(SLOTS):
                    shift_rows(b, g, s)
                    if s:
                        make_x1(b, g, s - 1)
                    elif not first:
                        make_x1(b, g - 1, SLOTS - 1)

            def pad_row(row):
                return ts(ring[:, row, :], ones[:, :], gmom[:, 0:1], None, ALU.mult)

            IMAGE_STEPS = 26
            with dve.Fori(0, B) as b:
                start_steps(b * IMAGE_STEPS + SETUP_STEPS)
                with dve.Fori(0, NG) as g:
                    count_x_group(b, g)
                wait_alone(dve, nth(b * NCH, 1 - NCH), x_counted)
                done(nc.vector.bn_aggr(mom, stats_x[:, :]))
                stt(out=mom[:, 1:2], in0=mom[:, 0:1], scalar=mom[:, 0:1], in1=mom[:, 1:2],
                    op0=ALU.mult, op1=ALU.add).then_inc(mom_ready, 1)
                normaliser(b * 2 + 1, b * 2 + 1)
                done(tt(scale0, center_w, rstd, ALU.mult))
                done(tt(scale0r, scale0, right, ALU.mult))
                done(tt(q0, wdw[:, :], rstd, ALU.mult))
                tt(q0, q0, gmom[:, 0:1], ALU.mult).then_inc(vec_ready, 1)
                ts(w_center[:, :], pwT[:, :], scale0, None, ALU.mult)
                ts(w_right[:, :], pwT[:, :], scale0r, None, ALU.mult)
                done(tt(pad_u, gmom[:, 0:1], inv_center_y, ALU.mult))
                for k in range(2):
                    for col in (0, W + 1):
                        ts(u_buf[k][:, :, col], ones[:, 0:ROWS], pad_u, None, ALU.mult)
                done(pad_row(0))
                dve.wait_ge(vec_done, b * 2 + 1)
                done(ts(bias0, ps_small[:, 4:5], -1.0, None, ALU.mult))
                ts(tmp, bias0, 1.0, None, ALU.mult).then_inc(shift_ready, 1)
                dve.wait_ge(shift_ready, b + 1)

                shift_group(b, 0, first=True)
                with dve.Fori(1, NG - 1) as g:
                    shift_group(b, g)
                dve.wait_ge(v_done, b * NCH + (NCH - SLOTS))
                done(pad_row(SLOTS * ROWS + 1))
                shift_group(b, NG - 1)
                make_x1(b, NG - 1, SLOTS - 1)

                dve.wait_ge(x1_ready, nth(b * NCH, 1 - NCH))
                dve.wait_ge(sq_done, nth(b * NCH, 1 - NCH))
                done(nc.vector.tensor_reduce(mom, sums_x1[:, :, :], mybir.AxisListType.X, ALU.add))
                ts(mom, mom, 1.0 / (H * W), None, ALU.mult).then_inc(mom_ready, 1)
                normaliser(b * 2 + 2, b * 2 + 2)
                tt(q1, rstd, gmom[:, 0:1], ALU.mult).then_inc(vec_ready, 1)
                done(ts(w_c1b[:, :, :], c1H[:, :, :], rstd, None, ALU.mult))
                dve.wait_ge(vec_done, b * 2 + 2)
                stt(out=bias1, in0=ps_small[:, 4:5], scalar=-2.0, in1=bc1[:, :],
                    op0=ALU.mult, op1=ALU.add).then_inc(c1_ready, 1)

                with dve.Fori(0, NG) as g:
                    for s in range(SLOTS):
                        t = b * NCH + g * SLOTS + s
                        dve.wait_ge(y1_ready, nth(t))
                        nc.vector.bn_stats(stats_y1[:, bass.ds(t * 6, 6)],
                                           y1_out[s // 2][:, (s % 2) * HC:(s % 2 + 1) * HC]
                                           ).then_inc(y1_counted, 1)
            assert steps[1] == IMAGE_STEPS

            start_steps(B * IMAGE_STEPS + SETUP_STEPS)
            dve.wait_ge(y1_counted, nth(B * NCH, 1))
            done(nc.vector.bn_aggr(mom, stats_y1[:, :]))
            done(ts(tmp, mom[:, 1:2], 1.0, None, ALU.mult))
            root(2 * B + 1)
            done(tt(h_scale, bn1[:, 0:1], rstd, ALU.mult))
            done(tt(tmp, mom[:, 0:1], h_scale, ALU.mult))
            tt(h_bias, bn1[:, 1:2], tmp, ALU.subtract)
            for k in range(2):
                dve.wait_ge(y1_stored[k], 16 * (B * NT // 2) + 16)
            for edge in (0, HH + 1):
                nc.vector.memset(h_pad[:, edge, :], 0.0)
            for edge in (0, HW + 1):
                nc.vector.memset(h_pad[:, 1:HH + 1, edge], 0.0)
            for k in range(2):
                last = nc.vector.memset(hT_buf[k][:, :, P], 1.0)
            last.then_inc(bn1_ready, 1)
            dve.wait_ge(bn1_ready, 1)
            MIDDLE = B * IMAGE_STEPS + SETUP_STEPS + steps[1]

            def dw_tile(b, j, last_tile=False):
                n = b * (2 * NT) + j * 2
                chain = b * (NT * 8) + j * 8
                dve.wait_ge(h_ready, nth(b * NT + j, 0 if last_tile else -1))
                for i, (dy, dx) in enumerate(DVE_TAPS):
                    for k in range(2):
                        o = o_all[:, bass.ds(j * TROWS + 4 * k, 4), :]
                        h = h_pad[:, bass.ds(j * TROWS + (4 * k + dy), 4), dx:dx + HW]
                        w = taps[:, 3 * dy + dx:3 * dy + dx + 1]
                        if i == 0:
                            dve.wait_ge(dw_done, nth(n + k))
                            stt(out=o, in0=h, scalar=w, in1=ps[:, 6 + k, :].rearrange("p (r c) -> p r c", c=HW),
                                op0=ALU.mult, op1=ALU.add).then_inc(dw_taken, 1)
                            continue
                        if i == 1:
                            dve.wait_ge(dw_taken, nth(n + k))
                        else:
                            dve.wait_ge(dw_acc, chain + (2 * (i - 2) + k + 1))
                        stt(out=o, in0=h, scalar=w, in1=o, op0=ALU.mult, op1=ALU.add).then_inc(dw_acc, 1)
                for k in range(2):
                    dve.wait_ge(dw_acc, chain + (6 + k + 1))
                    nc.vector.bn_stats(stats_o[:, bass.ds(j * 12 + 6 * k, 6)],
                                       o_all[:, bass.ds(j * TROWS + 4 * k, 4), :].rearrange("p r c -> p (r c)")
                                       ).then_inc(dw_counted, 1)

            PLANE_STEPS = 13
            with dve.Fori(0, B) as b:
                start_steps(b * PLANE_STEPS + MIDDLE)
                with dve.Fori(0, NT - 1) as j:
                    dw_tile(b, j)
                dw_tile(b, NT - 1, last_tile=True)
                wait_alone(dve, b * (2 * NT) + 2 * NT, dw_counted)
                done(nc.vector.bn_aggr(mom, stats_o[:, :]))
                done(tt(mom[:, 0:1], mom[:, 0:1], bdw[:, :], ALU.add))
                stt(out=mom[:, 1:2], in0=mom[:, 0:1], scalar=mom[:, 0:1], in1=mom[:, 1:2],
                    op0=ALU.mult, op1=ALU.add).then_inc(mom_ready, 1)
                normaliser(b + (2 * B + 1), b + (2 * B + 2))
                done(tt(ln_scale, rstd, gn[:, 0:1], ALU.mult))
                done(stt(out=ln_shift, in0=bdw[:, :], scalar=gmom[:, 0:1], in1=ln_scale,
                         op0=ALU.subtract, op1=ALU.mult))
                tt(ln_shift, ln_shift, gn[:, 1:2], ALU.add).then_inc(vec_ready, 1)
                done(ts(w_pw1b[:, :], pw1T[:, :], ln_scale, None, ALU.mult))
                dve.wait_ge(vec_done, b + (2 * B + 1))
                tt(bias_pw1, ps_small[:, 4:5], bpw1[:, :], ALU.add).then_inc(ln_ready, 1)

                with dve.Fori(0, NT) as j:
                    n = b * (2 * NT) + j * 2
                    for k in range(2):
                        dve.wait_ge(pw2_done, nth(n + k))
                        dve.wait_ge(h2_stored[k], b * (16 * NT) + j * 16 + 16)
                        dve.wait_ge(hT_done, nth(n + k, 2))
                        stt(out=h2_buf[k].rearrange("p (r c) -> p r c", c=HW),
                            in0=ps[:, 2 + k, :].rearrange("p (r c) -> p r c", c=HW), scalar=bpw2[:, :],
                            in1=h_pad[:, bass.ds(j * TROWS + (4 * k + 1), 4), 1:HW + 1],
                            op0=ALU.add, op1=ALU.add).then_inc(h2_ready, 1)
                    dve.wait_ge(gram_done, nth(b * NT + j))
                    dve.wait_ge(gram_added, nth(b * NT + j, 1))
                    tt(gram[:, :], gram[:, :], ps[:, 6, 0:P + 1], ALU.add).then_inc(gram_added, 1)
            assert steps[1] == PLANE_STEPS

            start_steps(MIDDLE + B * PLANE_STEPS)
            count = float(B * HH * HW)
            dve.wait_ge(gram_added, nth(B * NT, 1))
            ts(h2_mean, gram[:, P:P + 1], 1.0 / count, None, ALU.mult).then_inc(cov_ready, 1)
            dve.wait_ge(cov_done, 1)
            ts(h2_mean_row[:, 0, :], ps[0:1, 0, 0:P], -1.0, None, ALU.mult)
            nc.vector.tensor_copy(h2_mean_row[:, 1, :], ps[0:1, 0, 0:P]).then_inc(cov_ready, 1)
            dve.wait_ge(cov_done, 2)
            stt(out=gram[:, 0:P], in0=gram[:, 0:P], scalar=1.0 / count, in1=ps[:, 1, 0:P],
                op0=ALU.mult, op1=ALU.add).then_inc(cov_ready, 1)
            dve.wait_ge(cov_done, 3)
            tt(z_mean, ps[:, 3, 0:4], bc2[:, :], ALU.add)
            tt(cov_w[:, :, :], ps[:, 2, :].rearrange("p (q n) -> p q n", q=4), c2T[:, :, :],
               ALU.mult).then_inc(cov_ready, 1)
            dve.wait_ge(cov_done, 4)
            ts(z_tmp, ps[:, 4, 0:4], 0.0, EPS, ALU.max, ALU.add).then_inc(var_ready, 1)
            dve.wait_ge(std_ready, 3 * B + 2)
            refine(z_scale, z_std[:, :], z_tmp)
            done(tt(z_scale, z_scale, bn2[:, 0, :], ALU.mult))
            done(tt(z_bias, bc2[:, :], z_mean, ALU.subtract))
            done(tt(z_bias, z_bias, z_scale, ALU.mult))
            for k in range(2):
                dve.wait_ge(h2_stored[k], 16 * (B * NT) + 16)
            tt(z_bias, z_bias, bn2[:, 1, :], ALU.add).then_inc(bn2_ready, 1)

            with dve.Fori(0, B * NG) as g:
                for s in range(SLOTS):
                    t = g * SLOTS + s
                    k = s % 2
                    even, odd = g_buf[k][:, 0::2, :], g_buf[k][:, 1::2, :]
                    dve.wait_ge(g_ready, nth(t))
                    tt(s_buf[k][:, 0:2, :], even, odd, ALU.add)
                    tt(s_buf[k][:, 2:4, :], even, odd, ALU.subtract).then_inc(s_done, 1)
                    dve.wait_ge(s_done, nth(t))
                    dve.wait_ge(xe_loaded[s], g * 16 + 16)
                    cells = slot(s).rearrange("p (r a) c -> p a r c", a=2)
                    for a in range(2):
                        band = s_buf[k][:, 2 * a, :].rearrange("p (r c e) -> p r c e", r=ROWS // 2, e=1)
                        band = band.broadcast_to([P, ROWS // 2, HW, 2])
                        pair = cells[:, a, :, :].rearrange("p r (c e) -> p r c e", e=2)
                        stt(out=pair, in0=band, scalar=0.5, in1=pair, op0=ALU.mult,
                            op1=ALU.add).then_inc(halves_done, 1)
                    for a in range(2):
                        dve.wait_ge(halves_done, g * (2 * SLOTS) + (2 * s + a + 1))
                        band = s_buf[k][:, 2 * a + 1, :].rearrange("p (r c) -> p r c", c=HW)
                        pixels = cells[:, a, :, :].rearrange("p r (c e) -> p e r c", e=2)
                        for e in range(2):
                            last = stt(out=pixels[:, e], in0=band, scalar=0.5 - e, in1=pixels[:, e],
                                       op0=ALU.mult, op1=ALU.add)
                    last.then_inc(out_ready, 1)


def kernel(**inputs):
    import numpy as np
    import concourse.bacc as bacc
    from concourse.bass_utils import run_bass_kernel_spmd

    def arr(name):
        return np.asarray(inputs[name])

    def column(name):
        return arr(name).reshape(P, 1)

    L1 = "L1_conv_"
    laid = {
        "x": arr("x").reshape(B, P, H * W),
        "theta_s": arr("L0_conv_theta_s"),
        "w_dw": column("L0_conv_w_dw"),
        "w_pwT": arr("L0_conv_w_pw").T,
        "w_c1T": arr(L1 + "w_c1").reshape(P, 4, P).transpose(2, 1, 0),
        "b_c1": column(L1 + "b_c1"),
        "bn1_g": column(L1 + "bn1_g"),
        "bn1_b": column(L1 + "bn1_b"),
        "dw_w": arr(L1 + "dw_w").reshape(P, 9),
        "dw_b": column(L1 + "dw_b"),
        "gn_g": column(L1 + "gn_g"),
        "gn_b": column(L1 + "gn_b"),
        "pw1_wT": arr(L1 + "pw1_w").T,
        "pw1_b": column(L1 + "pw1_b"),
        "pw2_wT": arr(L1 + "pw2_w").T,
        "pw2_b": column(L1 + "pw2_b"),
        "w_c2T": arr(L1 + "w_c2").reshape(4, P, P).transpose(2, 0, 1),
        "b_c2": arr(L1 + "b_c2").reshape(4, P).T,
        "bn2_g": arr(L1 + "bn2_g").reshape(4, P).T,
        "bn2_b": arr(L1 + "bn2_b").reshape(4, P).T,
    }
    nc = bacc.Bacc("TRN2", target_bir_lowering=False, num_devices=1)
    feed, args = {}, {}
    for name, a in laid.items():
        a = np.ascontiguousarray(a)
        feed["in_" + name] = a
        args[name] = nc.dram_tensor("in_" + name, a.shape, mybir.dt.from_np(a.dtype), kind="ExternalInput").ap()
    args["out"] = nc.dram_tensor("out_x", (B, P, H * W), F32, kind="ExternalOutput").ap()
    preact_kernel(nc, **args)
    r = run_bass_kernel_spmd(nc, [feed], core_ids=[0])
    return r.results[0]["out_x"].reshape(B, P, H, W)
```

```python
from contextlib import ExitStack

import concourse.bass as bass
from concourse import mybir

F32 = mybir.dt.float32
BF16 = mybir.dt.bfloat16
ALU = mybir.AluOpType
ACT = mybir.ActivationFunctionType

P = 128
B, H, W = 8, 256, 256
HH, HW = H // 2, W // 2
G = 4
BANK = 512
ROWS = 8
CH = ROWS * W
NCH = H // ROWS
SLOTS = 4
NG = NCH // SLOTS
HC = CH // 4
TROWS = 8
TILE = TROWS * HW
NT = HH // TROWS
PE_TAPS = [(0, 0), (0, 1), (0, 2)]
DVE_TAPS = [(1, 0), (1, 1), (1, 2), (2, 0), (2, 1), (2, 2)]
ADDS = len(DVE_TAPS) - 1
DW_LAG = 2
SQ_LAG = 3
EPS = 1e-5
TINY = 2.0 ** -30
LEAD = 4

assert HC == BANK and NCH % SLOTS == 0 and TILE == 2 * BANK


def preact_kernel(nc, x, theta_s, w_dw, w_pwT, w_c1T, b_c1, bn1_g, bn1_b, dw_w, dw_b, gn_g, gn_b,
                  pw1_wT, pw1_b, pw2_wT, pw2_b, w_c2T, b_c2, bn2_g, bn2_b, out):
    x1_dram = nc.dram_tensor("x1_dram", (B * NCH, P, CH), F32, kind="Internal").ap()
    y1_dram = nc.dram_tensor("y1_dram", (B * NT, P, TILE), F32, kind="Internal").ap()
    h2_dram = nc.dram_tensor("h2_dram", (B * NT, P, TILE), F32, kind="Internal").ap()

    with ExitStack() as ctx:
        def sb(name, shape, dt=F32):
            return ctx.enter_context(nc.sbuf_tensor(name, shape, dt))

        def sem(name):
            return ctx.enter_context(nc.semaphore(name))

        ident = sb("ident", [P, P])
        group_mean = sb("group_mean", [P, P])
        all_mean = sb("all_mean", [P, P])
        ones = sb("ones", [P, W])
        theta = sb("theta", [P, 2])
        wdw = sb("wdw", [P, 1])
        pwT = sb("pwT", [P, P])
        c1T = sb("c1T", [P, 4, P])
        c1H = sb("c1H", [P, 4, P])
        bc1 = sb("bc1", [P, 1])
        bn1 = sb("bn1", [P, 2])
        taps = sb("taps", [P, 9])
        tap_diag = sb("tap_diag", [P, len(PE_TAPS), P])
        bdw = sb("bdw", [P, 1])
        gn = sb("gn", [P, 2])
        pw1T = sb("pw1T", [P, P])
        bpw1 = sb("bpw1", [P, 1])
        pw2T = sb("pw2T", [P, P])
        bpw2 = sb("bpw2", [P, 1])
        c2T = sb("c2T", [P, 4, P])
        bc2 = sb("bc2", [P, 4])
        bn2 = sb("bn2", [P, 2, 4])

        shift = sb("shift", [P, 8])
        center_y, center_x = shift[:, 0:1], shift[:, 1:2]
        up, left = shift[:, 2:3], shift[:, 3:4]
        down, right = shift[:, 4:5], shift[:, 5:6]
        center_w, inv_center_y = shift[:, 6:7], shift[:, 7:8]

        small = sb("small", [P, 40])
        mom = small[:, 0:2]
        gmom = small[:, 2:4]
        var, std, rstd, tmp = (small[:, k:k + 1] for k in range(4, 8))
        scale0, scale0r, q0, bias0 = (small[:, k:k + 1] for k in range(8, 12))
        pad_u = small[:, 12:13]
        q1, bias1, h_scale, h_bias = (small[:, k:k + 1] for k in range(13, 17))
        ln_scale, ln_shift, bias_pw1, h2_mean = (small[:, k:k + 1] for k in range(17, 21))
        z_mean, z_scale, z_bias = small[:, 21:25], small[:, 25:29], small[:, 29:33]
        z_tmp, z_std = small[:, 33:37], sb("z_std", [P, 4])
        h2_mean_row = sb("h2_mean_row", [1, 2, P])

        w_center = sb("w_center", [P, P])
        w_right = sb("w_right", [P, P])
        w_c1b = sb("w_c1b", [P, 4, P])
        w_pw1b = sb("w_pw1b", [P, P])
        stats_x = sb("stats_x", [P, NCH * 4 * 6])
        sums_x1 = sb("sums_x1", [P, 2, NCH])
        stats_y1 = sb("stats_y1", [P, B * NCH * 6])
        sums_o = sb("sums_o", [P, 2, NT * 2])
        warm = sb("warm", [P, 1])
        gram = sb("gram", [P, P + 1])
        cov_w = sb("cov_w", [P, 4, P])

        arena = sb("arena", [P, 38700])
        at = [0]

        def cut(n):
            at[0] += n
            assert at[0] <= 38700
            return arena[:, at[0] - n:at[0]]

        ring = cut((SLOTS * ROWS + 2) * W).rearrange("p (r c) -> p r c", c=W)
        u_buf = [cut(ROWS * (W + 2)).rearrange("p (r c) -> p r c", c=W + 2) for _ in range(2)]
        v_buf = [cut(CH) for _ in range(2)]
        x1_buf = [cut(CH) for _ in range(2)]
        ahead = [cut(CH) for _ in range(SLOTS)]
        squares = cut(CH // 2).bitcast(BF16)
        y1_out = [cut(TILE) for _ in range(2)]
        at[0] = 0
        h_pad = cut((HH + 2) * (HW + 2)).rearrange("p (r c) -> p r c", c=HW + 2)
        o_all = cut(HH * HW).rearrange("p (r c) -> p r c", c=HW)
        y1_in = o_in = [cut(TILE) for _ in range(2)]
        a_buf = [cut(BANK) for _ in range(2)]
        h2_buf = [cut(BANK) for _ in range(2)]
        hT_buf = [cut(4 * (P + 1)).rearrange("p (k c) -> p k c", k=4) for _ in range(2)]
        o_squares = cut(BANK // 2).bitcast(BF16)
        at[0] = (SLOTS * ROWS + 2) * W
        h2_in = [cut(TILE) for _ in range(2)]
        g_buf = [cut(4 * HC).rearrange("p (q n) -> p q n", q=4) for _ in range(2)]
        s_buf = [cut(4 * HC).rearrange("p (n r a c) -> p n r a c", n=2, a=2, c=HW) for _ in range(2)]

        ps = ctx.enter_context(nc.psum_tensor("ps", [P, 8, BANK], F32))
        ps_small = ps[:, 7, :]

        def banks(k):
            return ps[:, 4 * k:4 * k + 4, :].rearrange("p a n -> p (a n)")

        def slot(s, above=0, below=0):
            return ring[:, 1 + s * ROWS - above:1 + (s + 1) * ROWS + below, :]

        params_in = sem("params_in")
        passed = sem("passed")
        consts_made = sem("consts_made")
        setup_done = sem("setup_done")
        primed = sem("primed")
        dve_step = sem("dve_step")
        mom_ready, gmom_ready = sem("mom_ready"), sem("gmom_ready")
        var_ready, std_ready = sem("var_ready"), sem("std_ready")
        vec_ready, vec_done = sem("vec_ready"), sem("vec_done")
        shift_ready, c1_ready = sem("shift_ready"), sem("c1_ready")
        bn1_ready, ln_ready, bn2_ready = sem("bn1_ready"), sem("ln_ready"), sem("bn2_ready")
        cov_ready, cov_done = sem("cov_ready"), sem("cov_done")
        slot_in = [sem(f"slot_in{s}") for s in range(SLOTS)]
        ahead_in = [sem(f"ahead_in{s}") for s in range(SLOTS)]
        u_up, v_done = sem("u_up"), sem("v_done")
        dw_acc, warmed = sem("dw_acc"), sem("warmed")
        halves_done, out_ready = sem("halves_done"), sem("out_ready")
        y1_loaded = [sem(f"y1_loaded{k}") for k in range(2)]
        h2_loaded = [sem(f"h2_loaded{k}") for k in range(2)]
        xe_loaded = [sem(f"xe_loaded{s}") for s in range(SLOTS)]
        x_counted, x_in_psum, u_done = sem("x_counted"), sem("x_in_psum"), sem("u_done")
        conv_done, x1_ready, sq_done = sem("conv_done"), sem("x1_ready"), sem("sq_done")
        c1_done, y1_ready, y1_counted = sem("c1_done"), sem("y1_ready"), sem("y1_counted")
        h_ready, dw_done, dw_taken, o_squared = sem("h_ready"), sem("dw_done"), sem("dw_taken"), sem("o_squared")
        pw1_done, a_ready, pw2_done, h2_ready = sem("pw1_done"), sem("a_ready"), sem("pw2_done"), sem("h2_ready")
        hT_done, hT_ready = sem("hT_done"), sem("hT_ready")
        gram_done, gram_added = sem("gram_done"), sem("gram_added")
        c2_done, g_ready, s_done = sem("c2_done"), sem("g_ready"), sem("s_done")
        x1_stored = [sem(f"x1_stored{k}") for k in range(2)]
        y1_stored = [sem(f"y1_stored{k}") for k in range(2)]
        h2_stored = [sem(f"h2_stored{k}") for k in range(2)]
        out_stored = [sem(f"out_stored{s}") for s in range(SLOTS)]

        def nth(t, back=0):
            return t + (1 + LEAD - back)

        CONSTS = 7
        def adds(b, j):
            return b * (NT * 2 * ADDS) + j * (2 * ADDS)

        PARAMS = [(theta[:, :], theta_s), (wdw[:, :], w_dw), (pwT[:, :], w_pwT), (c1T[:, :, :], w_c1T),
                  (bc1[:, :], b_c1), (bn1[:, 0:1], bn1_g), (bn1[:, 1:2], bn1_b), (taps[:, :], dw_w),
                  (bdw[:, :], dw_b), (gn[:, 0:1], gn_g), (gn[:, 1:2], gn_b), (pw1T[:, :], pw1_wT),
                  (bpw1[:, :], pw1_b), (pw2T[:, :], pw2_wT), (bpw2[:, :], pw2_b), (c2T[:, :, :], w_c2T),
                  (bc2[:, :], b_c2), (bn2[:, 0, :], bn2_g), (bn2[:, 1, :], bn2_b)]

        def wait_alone(eng, value, *sems):
            for s_ in sems:
                eng.wait_ge(s_, value)
            eng.sem_inc(passed, 1)

        block = ctx.enter_context(nc.Block())

        @block.sync
        def _(sp):
            for dst, src in PARAMS:
                sp.dma_start(dst, src).then_inc(params_in, 16)

            def load_x_ahead(b, g, s):
                sp.wait_ge(x_counted, nth(b * NCH + g * SLOTS + s, SLOTS))
                sp.dma_start(ahead[s], x[b, :, bass.ds((g * SLOTS + s) * CH, CH)]).then_inc(ahead_in[s], 16)

            def load_ring(b, g, s, first=False, last=False):
                t = b * NCH + g * SLOTS + s
                above, below = int(s == 0 and not first), int(s == SLOTS - 1 and not last)
                wait_alone(sp, nth(t, SLOTS), x_in_psum)
                sp.wait_ge(u_done, nth(t, SLOTS if s == SLOTS - 1 else SLOTS - 1))
                sp.dma_start(slot(s, above, below),
                             x[b, :, bass.ds(((g * SLOTS + s) * ROWS - above) * W, (ROWS + above + below) * W)]
                             .rearrange("p (r c) -> p r c", c=W)).then_inc(slot_in[s], 16)

            def load_group(b, g, following, first=False, last=False):
                for s in range(SLOTS):
                    load_ring(b, g, s, first, last)
                    if following and not first:
                        load_x_ahead(b + 1, g, s)
                if following and first:
                    sp.wait_ge(c1_done, nth(b * NCH, 1))
                    for s in range(SLOTS):
                        load_x_ahead(b + 1, g, s)

            def load_image(b, following):
                load_group(b, 0, following, first=True)
                with sp.Fori(1, NG - 1) as g:
                    load_group(b, g, following)
                load_group(b, NG - 1, following, last=True)
                wait_alone(sp, nth((b + 1 + int(following)) * NCH, 1), x_counted)
                with sp.Fori(0, NG) as g:
                    for s in range(SLOTS):
                        wait_alone(sp, nth(b * NCH + g * SLOTS + s, SLOTS), c1_done)
                        sp.wait_ge(x1_stored[s % 2], b * (8 * NCH) + g * (8 * SLOTS) + (s // 2 * 16 + 32))
                        sp.dma_start(ahead[s], x1_dram[b * NCH + g * SLOTS + s]).then_inc(ahead_in[s], 16)

            with sp.Fori(0, NG) as g:
                for s in range(SLOTS):
                    load_x_ahead(0, g, s)
            with sp.Fori(0, B - 1) as b:
                load_image(b, following=True)
            load_image(B - 1, following=False)

            for k in range(2):
                sp.wait_ge(y1_stored[k], 16 * (B * NT // 2) + 16)
            sp.wait_ge(bn1_ready, 1)

            def planes_step(b, i, new, old):
                for k in range(2):
                    j = i * 2 + k
                    if new:
                        sp.wait_ge(h_ready, nth(b * NT + j, 2))
                        sp.dma_start(y1_in[k], y1_dram[b * NT + j]).then_inc(y1_loaded[k], 16)
                    if old:
                        for half in range(2):
                            sp.wait_ge(h2_ready, nth((b - 1) * (2 * NT) + j * 2 + half))
                            sp.dma_start(h2_dram[(b - 1) * NT + j, :, half * BANK:(half + 1) * BANK], h2_buf[half]
                                         ).then_inc(h2_stored[half], 16)

            def planes(b, new=True, old=True):
                with sp.Fori(0, NT // 2) as i:
                    planes_step(b, i, new, old)

            planes(0, old=False)
            with sp.Fori(1, B) as b:
                planes(b)
            planes(B, new=False)

            for k in range(2):
                sp.wait_ge(h2_stored[k], 16 * (B * NT) + 16)
            sp.wait_ge(bn2_ready, 1)

            def load_output_group(g):
                for s in range(SLOTS):
                    if s % 2 == 0:
                        sp.wait_ge(c2_done, nth(g * SLOTS + s, SLOTS - 1))
                        sp.dma_start(h2_in[s // 2], h2_dram[g * 2 + s // 2]).then_inc(h2_loaded[s // 2], 16)
                    if not isinstance(g, int):
                        sp.wait_ge(out_stored[s], g * 16)
                    sp.dma_start(slot(s), x1_dram[g * SLOTS + s].rearrange("p (r c) -> p r c", c=W)
                                 ).then_inc(xe_loaded[s], 16)

            load_output_group(0)
            with sp.Fori(1, B * NG) as g:
                load_output_group(g)
            for s in range(SLOTS):
                sp.wait_ge(out_stored[s], 16 * (B * NG))

        @block.gpsimd
        def _(pool):
            pool.memset(ident[:, :], 0.0).then_inc(consts_made, 1)
            pool.memset(group_mean[:, :], 1.0 / G).then_inc(consts_made, 1)
            pool.memset(all_mean[:, :], 1.0 / P).then_inc(consts_made, 1)
            pool.memset(ones[:, :], 1.0).then_inc(consts_made, 1)
            pool.wait_ge(consts_made, 4)
            pool.affine_select(out=ident[:, :], in_=ident[:, :], compare_op=ALU.not_equal, fill=1.0, base=0,
                               pattern=[[-1, P]], channel_multiplier=1).then_inc(consts_made, 1)
            groups = group_mean[:, :].rearrange("p (g c) -> p g c", c=G)
            pool.affine_select(out=groups, in_=groups, compare_op=ALU.is_ge, fill=0.0, base=0,
                               pattern=[[-G, P // G], [0, G]], channel_multiplier=1).then_inc(consts_made, 1)
            pool.wait_ge(consts_made, 6)
            pool.affine_select(out=groups, in_=groups, compare_op=ALU.is_ge, fill=0.0, base=G - 1,
                               pattern=[[G, P // G], [0, G]], channel_multiplier=-1).then_inc(consts_made, 1)
            with pool.Fori(0, B) as b:
                with pool.Fori(0, NG) as g:
                    for s in range(SLOTS):
                        pool.wait_ge(out_ready, b * NCH + g * SLOTS + (s + 1))
                        pool.dma_start(out[b, :, bass.ds((g * SLOTS + s) * CH, CH)]
                                       .rearrange("p (r c) -> p r c", c=W), slot(s)).then_inc(out_stored[s], 16)

        @block.scalar
        def _(act):
            for stored in x1_stored + y1_stored + h2_stored:
                act.sem_inc(stored, 16)
            for counter in (x_in_psum, x1_ready, sq_done, y1_ready, h_ready, a_ready, hT_ready, o_squared, g_ready):
                act.sem_inc(counter, LEAD)

            def square_root(n):
                act.wait_ge(var_ready, n)
                nc.scalar.activation(std, var, ACT.Sqrt).then_inc(std_ready, 1)

            def put_x(b, g, s):
                t = b * NCH + g * SLOTS + s
                k = s % 2
                act.wait_ge(slot_in[s], b * (16 * NG) + g * 16 + 16)
                act.wait_ge(x1_ready, nth(t, 2))
                nc.scalar.activation(banks(k), slot(s).rearrange("p r c -> p (r c)"), ACT.Identity,
                                     bias=bias0).then_inc(x_in_psum, 1)

            def take_x1(b, g, s):
                i = g * SLOTS + s
                t = b * NCH + i
                k = s % 2
                act.wait_ge(conv_done, nth(t))
                act.wait_ge(x1_stored[k], b * (8 * NCH) + g * (8 * SLOTS) + (s // 2 * 16 + 16))
                act.wait_ge(sq_done, nth(t, 2))
                nc.scalar.activation(x1_buf[k], banks(k), ACT.Identity,
                                     accum_out=sums_x1[:, 0, bass.ds(i, 1)]).then_inc(x1_ready, 1)
                act.wait_ge(x1_ready, nth(t))
                act.dma_start(x1_dram[t], x1_buf[k]).then_inc(x1_stored[k], 16)
                act.wait_ge(sq_done, nth(t, 1))
                nc.scalar.activation(squares, x1_buf[k], ACT.Square,
                                     accum_out=sums_x1[:, 1, bass.ds(i, 1)]).then_inc(sq_done, 1)

            def shift_group(b, g, first=False):
                for s in range(SLOTS):
                    put_x(b, g, s)
                    if s:
                        take_x1(b, g, s - 1)
                    elif not first:
                        take_x1(b, g - 1, SLOTS - 1)

            def y1_group(b, g):
                for s in range(SLOTS):
                    t = b * NCH + g * SLOTS + s
                    k = s // 2
                    act.wait_ge(c1_done, nth(t))
                    if s % 2 == 0:
                        act.wait_ge(y1_stored[k], b * (16 * NG) + g * 16 + 16)
                        act.wait_ge(y1_counted, nth(t, SLOTS - 1))
                    nc.scalar.activation(y1_out[k][:, (s % 2) * HC:(s % 2 + 1) * HC], ps[:, s, :],
                                         ACT.Identity, bias=bias1).then_inc(y1_ready, 1)
                    if s % 2 == 1:
                        act.wait_ge(y1_ready, nth(t))
                        act.dma_start(y1_dram[b * NT + g * 2 + k], y1_out[k]).then_inc(y1_stored[k], 16)

            with act.Fori(0, B) as b:
                square_root(b * 2 + 1)
                act.wait_ge(primed, b + 2)
                shift_group(b, 0, first=True)
                with act.Fori(1, NG) as g:
                    shift_group(b, g)
                take_x1(b, NG - 1, SLOTS - 1)
                square_root(b * 2 + 2)
                act.wait_ge(c1_ready, b + 1)
                with act.Fori(0, NG) as g:
                    y1_group(b, g)
            square_root(2 * B + 1)

            act.wait_ge(bn1_ready, 1)

            def square_o(b, j):
                for half in range(2):
                    act.wait_ge(dw_acc, adds(b, j) + ((ADDS - 1) * 2 + half + 1))
                    act.wait_ge(o_squared, nth(b * (2 * NT) + j * 2 + half, 1))
                    nc.scalar.activation(o_squares, o_all[:, bass.ds(j * TROWS + 4 * half, 4), :]
                                         .rearrange("p r c -> p (r c)"), ACT.Square,
                                         accum_out=sums_o[:, 1, bass.ds(j * 2 + half, 1)]).then_inc(o_squared, 1)

            def planes_step(b, i, new, old):
                for k in range(2):
                    j = i * 2 + k
                    n = (b - 1) * (2 * NT) + j * 2
                    if old:
                        for half in range(2):
                            act.wait_ge(pw1_done, nth(n + half))
                            act.wait_ge(pw2_done, nth(n + half, 2))
                            nc.scalar.activation(a_buf[half], ps[:, half, :], ACT.Gelu,
                                                 bias=bias_pw1).then_inc(a_ready, 1)
                    if new and not (isinstance(j, int) and j < SQ_LAG):
                        square_o(b, j - SQ_LAG)
                    if old:
                        act.wait_ge(h2_ready, nth(n + 1))
                    if new:
                        act.wait_ge(y1_loaded[k], b * (8 * NT) + i * 16 + 16)
                        nc.scalar.activation(h_pad[:, bass.ds(j * TROWS + 1, TROWS), 1:HW + 1],
                                             y1_in[k].rearrange("p (r c) -> p r c", c=HW), ACT.Gelu,
                                             bias=h_bias, scale=h_scale).then_inc(h_ready, 1)
                    if old:
                        for half in range(2):
                            act.wait_ge(hT_done, nth(n + half))
                            act.wait_ge(gram_done, nth((b - 1) * NT + j, 1))
                            nc.scalar.activation(hT_buf[half][:, :, 0:P],
                                                 ps[:, 4 + half, :].rearrange("p (k c) -> p k c", k=4),
                                                 ACT.Copy).then_inc(hT_ready, 1)

            def warm_gelu(n):
                act.wait_ge(warmed, n)
                nc.scalar.activation(warm[:, :], ones[:, 0:1], ACT.Gelu).then_inc(warmed, 1)

            def planes(b, new=True, old=True):
                warm_gelu(b)
                if old:
                    act.wait_ge(ln_ready, b)
                for i in range(2):
                    planes_step(b, i, new, old)
                with act.Fori(2, NT // 2) as i:
                    planes_step(b, i, new, old)
                if new:
                    for j in range(NT - SQ_LAG, NT):
                        square_o(b, j)
                    square_root(b + (2 * B + 2))

            planes(0, old=False)
            with act.Fori(1, B) as b:
                planes(b)
            planes(B, new=False)

            act.wait_ge(var_ready, 3 * B + 2)
            nc.scalar.activation(z_std[:, :], z_tmp, ACT.Sqrt).then_inc(std_ready, 1)
            warm_gelu(B + 1)
            act.wait_ge(bn2_ready, 1)
            with act.Fori(0, B * NCH // 2) as i:
                for k in range(2):
                    act.wait_ge(c2_done, nth(i * 2 + k))
                    act.wait_ge(s_done, nth(i * 2 + k, 2))
                    for q in range(4):
                        last = nc.scalar.activation(g_buf[k][:, q, :], ps[:, 4 * k + q, :], ACT.Gelu,
                                                    bias=z_bias[:, q:q + 1], scale=z_scale[:, q:q + 1])
                    last.then_inc(g_ready, 1)

        @block.tensor
        def _(pe):
            mm = nc.tensor.matmul
            for counter in (conv_done, c1_done, dw_done, pw1_done, pw2_done, hT_done, gram_done, c2_done):
                pe.sem_inc(counter, LEAD)

            def channel_means(n, weights):
                pe.wait_ge(mom_ready, n)
                mm(ps_small[:, 0:2], weights[:, :], mom, start=True, stop=True).then_inc(gmom_ready, 1)

            def vector_product(n, weights, vec):
                pe.wait_ge(vec_ready, n)
                mm(ps_small[:, 4:5], weights, vec, start=True, stop=True).then_inc(vec_done, 1)

            def shift_group(b, g):
                for s in range(SLOTS):
                    t = b * NCH + g * SLOTS + s
                    k = s % 2
                    pe.wait_ge(v_done, t + 1)
                    pe.wait_ge(x_in_psum, nth(t))
                    for r in range(4):
                        mm(ps[:, 4 * k + r, :], w_center[:, :], v_buf[k][:, r * BANK:(r + 1) * BANK],
                           start=False, stop=False, skip_group_check=True)
                        last = mm(ps[:, 4 * k + r, :], w_right[:, :], u_buf[k][:, 2 * r:2 * r + 2, 2:W + 2],
                                  start=False, stop=True, skip_group_check=True)
                    last.then_inc(conv_done, 1)

            def c1_group(b, g, last_image):
                for s in range(SLOTS):
                    t = b * NCH + g * SLOTS + s
                    pe.wait_ge(ahead_in[s], b * (32 * NG) + g * 16 + ((16 if last_image else 32) * NG + 16))
                    pe.wait_ge(y1_ready, nth(t, SLOTS))
                    cells = ahead[s].rearrange("p (r a c e) -> p a e r c", a=2, c=HW, e=2)
                    for q in range(4):
                        last = mm(ps[:, s, :], w_c1b[:, q, :], cells[:, q // 2, q % 2, :, :],
                                  start=(q == 0), stop=(q == 3))
                    last.then_inc(c1_done, 1)

            def prime(bank):
                return mm(ps[:, bank, :], ident[:, :], c2T[:, :, :], start=True, stop=True)

            def image(b, last_image=False):
                channel_means(b * 2 + 1, group_mean)
                vector_product(b * 2 + 1, pwT[:, :], q0)
                pe.wait_ge(shift_ready, b + 1)
                prime(7).then_inc(primed, 1)
                pe.wait_ge(primed, b + 2)
                shift_group(b, 0)
                with pe.Fori(1, NG) as g:
                    shift_group(b, g)
                channel_means(b * 2 + 2, group_mean)
                vector_product(b * 2 + 2, c1T[:, 0, :], q1)
                wait_alone(pe, b + 1, c1_ready)
                with pe.Fori(0, NG) as g:
                    c1_group(b, g, last_image)

            pe.wait_ge(setup_done, 1)
            for bank in range(7):
                last = prime(bank)
            last.then_inc(primed, 1)
            with pe.Fori(0, B - 1) as b:
                image(b)
            image(B - 1, last_image=True)

            def first_conv(b, j, back):
                n = b * (2 * NT) + j * 2
                pe.wait_ge(gram_added, nth(b * NT + j, back))
                for half in range(2):
                    pe.wait_ge(a_ready, nth(n + half, 2))
                    mm(ps[:, half, :], w_pw1b[:, :], o_all[:, bass.ds(j * TROWS + 4 * half, 4), :],
                       start=True, stop=True).then_inc(pw1_done, 1)

            def second_conv(b, j):
                n = b * (2 * NT) + j * 2
                for half in range(2):
                    pe.wait_ge(a_ready, nth(n + half))
                    pe.wait_ge(h2_ready, nth(n + half, 2))
                    mm(ps[:, 2 + half, :], pw2T[:, :], a_buf[half], start=True, stop=True).then_inc(pw2_done, 1)

            def turn_h2(b, j):
                n = b * (2 * NT) + j * 2
                for half in range(2):
                    pe.wait_ge(h2_ready, nth(n + half))
                    pe.wait_ge(hT_ready, nth(n + half, 2))
                    for c in range(4):
                        last = nc.tensor.transpose(ps[:, 4 + half, c * P:(c + 1) * P],
                                                   h2_buf[half][:, c * P:(c + 1) * P], ident[:, :])
                    last.then_inc(hT_done, 1)

            def gram_tile(b, j):
                n = b * (2 * NT) + j * 2
                pe.wait_ge(gram_added, nth(b * NT + j, 1))
                for half in range(2):
                    pe.wait_ge(hT_ready, nth(n + half))
                    for c in range(4):
                        last = mm(ps[:, 0, 0:P + 1], hT_buf[half][:, c, 0:P], hT_buf[half][:, c, :],
                                  start=(half == 0 and c == 0), stop=(half == 1 and c == 3))
                last.then_inc(gram_done, 1)

            def dw_half(b, j, half, last_tile=False):
                pe.wait_ge(h_ready, nth(b * NT + j, 0 if last_tile else -1))
                pe.wait_ge(dw_taken, nth(b * (2 * NT) + j * 2 + half, 2))
                for n, (dy, dx) in enumerate(PE_TAPS):
                    last = mm(ps[:, 6 + half, :], tap_diag[:, n, :],
                              h_pad[:, bass.ds(j * TROWS + (4 * half + dy), 4), dx:dx + HW],
                              start=(n == 0), stop=(n == len(PE_TAPS) - 1))
                last.then_inc(dw_done, 1)

            def planes_step(b, j, new, old):
                early = isinstance(j, int)
                if old:
                    first_conv(b - 1, j, back=1 if early and j == 0 else 2)
                if new and not early:
                    dw_half(b, j - DW_LAG, 0)
                    dw_half(b, j - DW_LAG, 1)
                if old:
                    second_conv(b - 1, j)
                if old and not (early and j == 0):
                    gram_tile(b - 1, j - 1)
                if old:
                    turn_h2(b - 1, j)

            def planes(b, new=True, old=True):
                if old:
                    pe.wait_ge(ln_ready, b)
                for j in range(DW_LAG):
                    planes_step(b, j, new, old)
                with pe.Fori(DW_LAG, NT) as j:
                    planes_step(b, j, new, old)
                if old:
                    gram_tile(b - 1, NT - 1)
                if new:
                    for j in range(NT - DW_LAG, NT):
                        for half in range(2):
                            dw_half(b, j, half, last_tile=(j == NT - 1))
                    channel_means(b + (2 * B + 1), all_mean)
                    vector_product(b + (2 * B + 1), pw1T[:, :], ln_shift)

            pe.wait_ge(bn1_ready, 1)
            planes(0, old=False)
            with pe.Fori(1, B) as b:
                planes(b)
            planes(B, new=False)

            pe.wait_ge(cov_ready, 1)
            mm(ps[0:1, 0, 0:P], h2_mean, ident[:, :], start=True, stop=True).then_inc(cov_done, 1)
            pe.wait_ge(cov_ready, 2)
            mm(ps[:, 1, 0:P], h2_mean_row[:, 0, :], h2_mean_row[:, 1, :], start=True, stop=True).then_inc(cov_done, 1)
            pe.wait_ge(cov_ready, 3)
            mm(ps[:, 2, :], gram[:, 0:P], c2T[:, :, :], start=True, stop=True)
            for q in range(4):
                last = mm(ps[:, 3, q:q + 1], c2T[:, q, :], h2_mean, start=True, stop=True)
            last.then_inc(cov_done, 1)
            pe.wait_ge(cov_ready, 4)
            for q in range(4):
                last = mm(ps[:, 4, q:q + 1], cov_w[:, q, :], ones[:, 0:1], start=True, stop=True)
            last.then_inc(cov_done, 1)

            pe.wait_ge(bn2_ready, 1)
            with pe.Fori(0, B * NG) as g:
                for s in range(SLOTS):
                    k = s % 2
                    if k == 0:
                        pe.wait_ge(h2_loaded[s // 2], g * 16 + 16)
                    pe.wait_ge(g_ready, nth(g * SLOTS + s, 2))
                    for q in range(4):
                        last = mm(ps[:, 4 * k + q, :], c2T[:, q, :], h2_in[s // 2][:, k * HC:(k + 1) * HC],
                                  start=True, stop=True)
                    last.then_inc(c2_done, 1)

        @block.vector
        def _(dve):
            stt, ts, tt = nc.vector.scalar_tensor_tensor, nc.vector.tensor_scalar, nc.vector.tensor_tensor
            for counter in (x_counted, u_done, y1_counted, dw_taken, h2_ready, gram_added, s_done):
                dve.sem_inc(counter, LEAD)

            steps = [0, 0]

            def start_steps(base):
                steps[0], steps[1] = base, 0

            def done(ins):
                steps[1] += 1
                ins.then_inc(dve_step, 1)
                dve.wait_ge(dve_step, steps[0] + steps[1])

            def refine(r, s, v):
                done(nc.vector.reciprocal(r, s))
                done(tt(s, r, r, ALU.mult))
                done(tt(s, s, v, ALU.mult))
                done(ts(s, s, -0.5, 1.5, ALU.mult, ALU.add))
                done(tt(r, r, s, ALU.mult))

            def normaliser(n, nth_root):
                dve.wait_ge(gmom_ready, n)
                done(nc.vector.tensor_copy(gmom, ps_small[:, 0:2]))
                done(stt(out=tmp, in0=gmom[:, 0:1], scalar=gmom[:, 0:1], in1=gmom[:, 1:2],
                         op0=ALU.mult, op1=ALU.subtract))
                done(ts(tmp, tmp, 0.0, -1.0, ALU.min, ALU.mult))
                root(nth_root)

            def root(n):
                ts(var, tmp, EPS, None, ALU.add).then_inc(var_ready, 1)
                dve.wait_ge(std_ready, n)
                refine(rstd, std, var)

            dve.wait_ge(params_in, 16 * len(PARAMS))
            dve.wait_ge(consts_made, CONSTS)
            start_steps(0)
            for axis, center, inverse, before, after in ((0, center_y, inv_center_y, up, down),
                                                         (1, center_x, center_w, left, right)):
                th = theta[:, axis:axis + 1]
                done(ts(tmp, th, -1.0, None, ALU.mult))
                done(tt(center, th, tmp, ALU.max))
                done(ts(center, center, -1.0, 1.0, ALU.mult, ALU.add))
                done(ts(center, center, TINY, None, ALU.max))
                done(nc.vector.reciprocal(inverse, center))
                done(ts(before, th, 0.0, None, ALU.max))
                done(tt(before, before, inverse, ALU.mult))
                done(ts(after, tmp, 0.0, None, ALU.max))
                done(tt(after, after, inverse, ALU.mult))
            done(tt(center_w, center_y, center_x, ALU.mult))
            done(tt(center_w, center_w, wdw[:, :], ALU.mult))
            ll, lh, hl, hh = (c1T[:, q, :] for q in range(4))
            tt(cov_w[:, 0, :], ll, lh, ALU.add)
            tt(cov_w[:, 1, :], ll, lh, ALU.subtract)
            tt(cov_w[:, 2, :], hl, hh, ALU.add)
            done(tt(cov_w[:, 3, :], hl, hh, ALU.subtract))
            tt(c1H[:, 0, :], cov_w[:, 0, :], cov_w[:, 2, :], ALU.add)
            tt(c1H[:, 1, :], cov_w[:, 0, :], cov_w[:, 2, :], ALU.subtract)
            tt(c1H[:, 2, :], cov_w[:, 1, :], cov_w[:, 3, :], ALU.add)
            done(tt(c1H[:, 3, :], cov_w[:, 1, :], cov_w[:, 3, :], ALU.subtract))
            done(ts(c1H[:, :, :], c1H[:, :, :], 0.5, None, ALU.mult))
            for n, (dy, dx) in enumerate(PE_TAPS):
                ts(tap_diag[:, n, :], ident[:, :], taps[:, 3 * dy + dx:3 * dy + dx + 1], None, ALU.mult)
            nc.vector.memset(gram[:, :], 0.0).then_inc(setup_done, 1)
            dve.wait_ge(setup_done, 1)
            SETUP_STEPS = 23
            assert steps[1] == SETUP_STEPS

            def count_x(b, g, s, pieces=range(4)):
                seen = g * 16 + 16 if isinstance(b, int) else (b - 1) * (32 * NG) + g * 16 + (16 * NG + 16)
                if 0 in pieces:
                    dve.wait_ge(ahead_in[s], seen)
                for r in pieces:
                    last = nc.vector.bn_stats(stats_x[:, bass.ds((g * SLOTS + s) * 24 + 6 * r, 6)],
                                              ahead[s][:, r * BANK:(r + 1) * BANK])
                if 3 in pieces:
                    last.then_inc(x_counted, 1)

            def shift_rows(b, g, s, following):
                t = b * NCH + g * SLOTS + s
                k = s % 2
                for near in range(s, min(s + 2, SLOTS)):
                    dve.wait_ge(slot_in[near], b * (16 * NG) + g * 16 + 16)
                dve.wait_ge(conv_done, nth(t, 2))
                u = u_buf[k][:, :, 1:W + 1]
                stt(out=u, in0=ring[:, s * ROWS:(s + 1) * ROWS, :], scalar=up, in1=slot(s),
                    op0=ALU.mult, op1=ALU.add).then_inc(u_up, 1)
                if following:
                    count_x(b + 1, g, s, range(0, 2))
                dve.wait_ge(u_up, t + 1)
                stt(out=u, in0=ring[:, s * ROWS + 2:(s + 1) * ROWS + 2, :], scalar=down, in1=u,
                    op0=ALU.mult, op1=ALU.add).then_inc(u_done, 1)
                if following:
                    count_x(b + 1, g, s, range(2, 4))
                dve.wait_ge(u_done, nth(t))
                stt(out=v_buf[k].rearrange("p (r c) -> p r c", c=W), in0=u_buf[k][:, :, 0:W], scalar=left, in1=u,
                    op0=ALU.mult, op1=ALU.add).then_inc(v_done, 1)

            def shift_group(b, g, following):
                for s in range(SLOTS):
                    shift_rows(b, g, s, following)

            def pad_row(row):
                return ts(ring[:, row, :], ones[:, :], gmom[:, 0:1], None, ALU.mult)

            IMAGE_STEPS = 26

            def image(b, following=True):
                start_steps(b * IMAGE_STEPS + SETUP_STEPS)
                wait_alone(dve, nth(b * NCH, 1 - NCH), x_counted)
                done(nc.vector.bn_aggr(mom, stats_x[:, :]))
                stt(out=mom[:, 1:2], in0=mom[:, 0:1], scalar=mom[:, 0:1], in1=mom[:, 1:2],
                    op0=ALU.mult, op1=ALU.add).then_inc(mom_ready, 1)
                normaliser(b * 2 + 1, b * 2 + 1)
                done(tt(scale0, center_w, rstd, ALU.mult))
                done(tt(scale0r, scale0, right, ALU.mult))
                done(tt(q0, wdw[:, :], rstd, ALU.mult))
                tt(q0, q0, gmom[:, 0:1], ALU.mult).then_inc(vec_ready, 1)
                ts(w_center[:, :], pwT[:, :], scale0, None, ALU.mult)
                ts(w_right[:, :], pwT[:, :], scale0r, None, ALU.mult)
                done(tt(pad_u, gmom[:, 0:1], inv_center_y, ALU.mult))
                for k in range(2):
                    for col in (0, W + 1):
                        ts(u_buf[k][:, :, col], ones[:, 0:ROWS], pad_u, None, ALU.mult)
                done(pad_row(0))
                dve.wait_ge(vec_done, b * 2 + 1)
                done(ts(bias0, ps_small[:, 4:5], -1.0, None, ALU.mult))
                ts(tmp, bias0, 1.0, None, ALU.mult).then_inc(shift_ready, 1)
                wait_alone(dve, b + 1, shift_ready)

                with dve.Fori(0, NG - 1) as g:
                    shift_group(b, g, following)
                done(pad_row(SLOTS * ROWS + 1))
                shift_group(b, NG - 1, following)

                dve.wait_ge(x1_ready, nth(b * NCH, 1 - NCH))
                dve.wait_ge(sq_done, nth(b * NCH, 1 - NCH))
                done(nc.vector.tensor_reduce(mom, sums_x1[:, :, :], mybir.AxisListType.X, ALU.add))
                ts(mom, mom, 1.0 / (H * W), None, ALU.mult).then_inc(mom_ready, 1)
                normaliser(b * 2 + 2, b * 2 + 2)
                tt(q1, rstd, gmom[:, 0:1], ALU.mult).then_inc(vec_ready, 1)
                done(ts(w_c1b[:, :, :], c1H[:, :, :], rstd, None, ALU.mult))
                dve.wait_ge(vec_done, b * 2 + 2)
                stt(out=bias1, in0=ps_small[:, 4:5], scalar=-2.0, in1=bc1[:, :],
                    op0=ALU.mult, op1=ALU.add).then_inc(c1_ready, 1)

                with dve.Fori(0, NG) as g:
                    for s in range(SLOTS):
                        t = b * NCH + g * SLOTS + s
                        dve.wait_ge(y1_ready, nth(t))
                        nc.vector.bn_stats(stats_y1[:, bass.ds(t * 6, 6)],
                                           y1_out[s // 2][:, (s % 2) * HC:(s % 2 + 1) * HC]
                                           ).then_inc(y1_counted, 1)

            with dve.Fori(0, NG) as g:
                for s in range(SLOTS):
                    count_x(0, g, s)
            with dve.Fori(0, B - 1) as b:
                image(b)
            image(B - 1, following=False)
            assert steps[1] == IMAGE_STEPS

            start_steps(B * IMAGE_STEPS + SETUP_STEPS)
            dve.wait_ge(y1_counted, nth(B * NCH, 1))
            done(nc.vector.bn_aggr(mom, stats_y1[:, :]))
            done(ts(tmp, mom[:, 1:2], 1.0, None, ALU.mult))
            root(2 * B + 1)
            done(tt(h_scale, bn1[:, 0:1], rstd, ALU.mult))
            done(tt(tmp, mom[:, 0:1], h_scale, ALU.mult))
            tt(h_bias, bn1[:, 1:2], tmp, ALU.subtract)
            for k in range(2):
                dve.wait_ge(y1_stored[k], 16 * (B * NT // 2) + 16)
            for edge in (0, HH + 1):
                nc.vector.memset(h_pad[:, edge, :], 0.0)
            for edge in (0, HW + 1):
                nc.vector.memset(h_pad[:, 1:HH + 1, edge], 0.0)
            for k in range(2):
                last = nc.vector.memset(hT_buf[k][:, :, P], 1.0)
            last.then_inc(bn1_ready, 1)
            dve.wait_ge(bn1_ready, 1)
            MIDDLE = B * IMAGE_STEPS + SETUP_STEPS + steps[1]

            def make_h2(b, j):
                for half in range(2):
                    n = b * (2 * NT) + j * 2 + half
                    dve.wait_ge(pw2_done, nth(n))
                    dve.wait_ge(h2_stored[half], b * (16 * NT) + j * 16 + 16)
                    dve.wait_ge(hT_done, nth(n, 2))
                    stt(out=h2_buf[half].rearrange("p (r c) -> p r c", c=HW),
                        in0=ps[:, 2 + half, :].rearrange("p (r c) -> p r c", c=HW), scalar=bpw2[:, :],
                        in1=h_pad[:, bass.ds(j * TROWS + (4 * half + 1), 4), 1:HW + 1],
                        op0=ALU.add, op1=ALU.add).then_inc(h2_ready, 1)

            def add_taps(b, j, first, end, last_tile=False):
                if first == 0:
                    dve.wait_ge(h_ready, nth(b * NT + j, 0 if last_tile else -1))
                for i in range(first, end):
                    dy, dx = DVE_TAPS[i]
                    w = taps[:, 3 * dy + dx:3 * dy + dx + 1]
                    for half in range(2):
                        n = b * (2 * NT) + j * 2 + half
                        o = o_all[:, bass.ds(j * TROWS + 4 * half, 4), :]
                        h = h_pad[:, bass.ds(j * TROWS + (4 * half + dy), 4), dx:dx + HW]
                        if i == 0:
                            dve.wait_ge(dw_done, nth(n))
                            stt(out=o, in0=h, scalar=w, in1=ps[:, 6 + half, :].rearrange("p (r c) -> p r c", c=HW),
                                op0=ALU.mult, op1=ALU.add).then_inc(dw_taken, 1)
                            continue
                        if i == 1:
                            dve.wait_ge(dw_taken, nth(n))
                        else:
                            dve.wait_ge(dw_acc, adds(b, j) + (2 * (i - 2) + half + 1))
                        total = sums_o[:, 0, bass.ds(j * 2 + half, 1)] if i == ADDS else None
                        stt(out=o, in0=h, scalar=w, in1=o, op0=ALU.mult, op1=ALU.add,
                            accum_out=total).then_inc(dw_acc, 1)

            def add_gram(b, j):
                dve.wait_ge(gram_done, nth(b * NT + j))
                dve.wait_ge(gram_added, nth(b * NT + j, 1))
                tt(gram[:, :], gram[:, :], ps[:, 0, 0:P + 1], ALU.add).then_inc(gram_added, 1)

            def planes_step(b, j, new, old):
                early = isinstance(j, int)
                taps_now = new and not early
                if taps_now:
                    add_taps(b, j - DW_LAG, 0, 2)
                if old:
                    make_h2(b - 1, j)
                if taps_now:
                    add_taps(b, j - DW_LAG, 2, 3)
                if old and not (early and j == 0):
                    add_gram(b - 1, j - 1)
                if taps_now:
                    add_taps(b, j - DW_LAG, 3, ADDS + 1)

            PLANE_STEPS = 15

            def planes(b, new=True, old=True):
                for j in range(DW_LAG):
                    planes_step(b, j, new, old)
                with dve.Fori(DW_LAG, NT) as j:
                    planes_step(b, j, new, old)
                if old:
                    add_gram(b - 1, NT - 1)
                if not new:
                    return
                for j in range(NT - DW_LAG, NT):
                    add_taps(b, j, 0, ADDS + 1, last_tile=(j == NT - 1))
                start_steps(b * PLANE_STEPS + MIDDLE)
                dve.wait_ge(dw_acc, adds(b, NT))
                dve.wait_ge(o_squared, nth(b * (2 * NT), 1 - 2 * NT))
                done(nc.vector.tensor_reduce(mom, sums_o[:, :, :], mybir.AxisListType.X, ALU.add))
                done(ts(mom, mom, 1.0 / (HH * HW), None, ALU.mult))
                done(stt(out=tmp, in0=mom[:, 0:1], scalar=mom[:, 0:1], in1=mom[:, 1:2],
                         op0=ALU.mult, op1=ALU.subtract))
                done(tt(mom[:, 0:1], mom[:, 0:1], bdw[:, :], ALU.add))
                stt(out=mom[:, 1:2], in0=mom[:, 0:1], scalar=mom[:, 0:1], in1=tmp,
                    op0=ALU.mult, op1=ALU.subtract).then_inc(mom_ready, 1)
                normaliser(b + (2 * B + 1), b + (2 * B + 2))
                done(tt(ln_scale, rstd, gn[:, 0:1], ALU.mult))
                done(stt(out=ln_shift, in0=bdw[:, :], scalar=gmom[:, 0:1], in1=ln_scale,
                         op0=ALU.subtract, op1=ALU.mult))
                tt(ln_shift, ln_shift, gn[:, 1:2], ALU.add).then_inc(vec_ready, 1)
                done(ts(w_pw1b[:, :], pw1T[:, :], ln_scale, None, ALU.mult))
                dve.wait_ge(vec_done, b + (2 * B + 1))
                tt(bias_pw1, ps_small[:, 4:5], bpw1[:, :], ALU.add).then_inc(ln_ready, 1)


            planes(0, old=False)
            with dve.Fori(1, B) as b:
                planes(b)
            planes(B, new=False)
            assert steps[1] == PLANE_STEPS

            start_steps(MIDDLE + B * PLANE_STEPS)
            count = float(B * HH * HW)
            dve.wait_ge(gram_added, nth(B * NT, 1))
            ts(h2_mean, gram[:, P:P + 1], 1.0 / count, None, ALU.mult).then_inc(cov_ready, 1)
            dve.wait_ge(cov_done, 1)
            ts(h2_mean_row[:, 0, :], ps[0:1, 0, 0:P], -1.0, None, ALU.mult)
            nc.vector.tensor_copy(h2_mean_row[:, 1, :], ps[0:1, 0, 0:P]).then_inc(cov_ready, 1)
            dve.wait_ge(cov_done, 2)
            stt(out=gram[:, 0:P], in0=gram[:, 0:P], scalar=1.0 / count, in1=ps[:, 1, 0:P],
                op0=ALU.mult, op1=ALU.add).then_inc(cov_ready, 1)
            dve.wait_ge(cov_done, 3)
            tt(z_mean, ps[:, 3, 0:4], bc2[:, :], ALU.add)
            tt(cov_w[:, :, :], ps[:, 2, :].rearrange("p (q n) -> p q n", q=4), c2T[:, :, :],
               ALU.mult).then_inc(cov_ready, 1)
            dve.wait_ge(cov_done, 4)
            ts(z_tmp, ps[:, 4, 0:4], 0.0, EPS, ALU.max, ALU.add).then_inc(var_ready, 1)
            dve.wait_ge(std_ready, 3 * B + 2)
            refine(z_scale, z_std[:, :], z_tmp)
            done(tt(z_scale, z_scale, bn2[:, 0, :], ALU.mult))
            done(tt(z_bias, bc2[:, :], z_mean, ALU.subtract))
            done(tt(z_bias, z_bias, z_scale, ALU.mult))
            for k in range(2):
                dve.wait_ge(h2_stored[k], 16 * (B * NT) + 16)
            tt(z_bias, z_bias, bn2[:, 1, :], ALU.add).then_inc(bn2_ready, 1)

            with dve.Fori(0, B * NG) as g:
                for s in range(SLOTS):
                    t = g * SLOTS + s
                    k = s % 2
                    even, odd = (g_buf[k][:, q::2, :].rearrange("p q (r c) -> p q r c", c=HW) for q in range(2))
                    dve.wait_ge(g_ready, nth(t))
                    tt(s_buf[k][:, :, :, 0, :], even, odd, ALU.add)
                    tt(s_buf[k][:, :, :, 1, :], even, odd, ALU.subtract).then_inc(s_done, 1)
                    dve.wait_ge(s_done, nth(t))
                    dve.wait_ge(xe_loaded[s], g * 16 + 16)
                    pairs = slot(s).rearrange("p r (c e) -> p (r c) e", e=2)
                    low, high = (s_buf[k][:, n].rearrange("p r a c -> p (r a c)") for n in range(2))
                    stt(out=pairs, in0=low.rearrange("p (n e) -> p n e", e=1).broadcast_to([P, CH // 2, 2]),
                        scalar=0.5, in1=pairs, op0=ALU.mult, op1=ALU.add).then_inc(halves_done, 1)
                    dve.wait_ge(halves_done, t + 1)
                    for e in range(2):
                        last = stt(out=pairs[:, :, e], in0=high, scalar=0.5 - e, in1=pairs[:, :, e],
                                   op0=ALU.mult, op1=ALU.add)
                    last.then_inc(out_ready, 1)


def kernel(**inputs):
    import numpy as np
    import concourse.bacc as bacc
    from concourse.bass_utils import run_bass_kernel_spmd

    def arr(name):
        return np.asarray(inputs[name])

    def column(name):
        return arr(name).reshape(P, 1)

    L1 = "L1_conv_"
    laid = {
        "x": arr("x").reshape(B, P, H * W),
        "theta_s": arr("L0_conv_theta_s"),
        "w_dw": column("L0_conv_w_dw"),
        "w_pwT": arr("L0_conv_w_pw").T,
        "w_c1T": arr(L1 + "w_c1").reshape(P, 4, P).transpose(2, 1, 0),
        "b_c1": column(L1 + "b_c1"),
        "bn1_g": column(L1 + "bn1_g"),
        "bn1_b": column(L1 + "bn1_b"),
        "dw_w": arr(L1 + "dw_w").reshape(P, 9),
        "dw_b": column(L1 + "dw_b"),
        "gn_g": column(L1 + "gn_g"),
        "gn_b": column(L1 + "gn_b"),
        "pw1_wT": arr(L1 + "pw1_w").T,
        "pw1_b": column(L1 + "pw1_b"),
        "pw2_wT": arr(L1 + "pw2_w").T,
        "pw2_b": column(L1 + "pw2_b"),
        "w_c2T": arr(L1 + "w_c2").reshape(4, P, P).transpose(2, 0, 1),
        "b_c2": arr(L1 + "b_c2").reshape(4, P).T,
        "bn2_g": arr(L1 + "bn2_g").reshape(4, P).T,
        "bn2_b": arr(L1 + "bn2_b").reshape(4, P).T,
    }
    nc = bacc.Bacc("TRN2", target_bir_lowering=False, num_devices=1)
    feed, args = {}, {}
    for name, a in laid.items():
        a = np.ascontiguousarray(a)
        feed["in_" + name] = a
        args[name] = nc.dram_tensor("in_" + name, a.shape, mybir.dt.from_np(a.dtype), kind="ExternalInput").ap()
    args["out"] = nc.dram_tensor("out_x", (B, P, H * W), F32, kind="ExternalOutput").ap()
    preact_kernel(nc, **args)
    r = run_bass_kernel_spmd(nc, [feed], core_ids=[0])
    return r.results[0]["out_x"].reshape(B, P, H, W)
```

```python
from contextlib import ExitStack

import concourse.bass as bass
from concourse import mybir

F32 = mybir.dt.float32
BF16 = mybir.dt.bfloat16
ALU = mybir.AluOpType
ACT = mybir.ActivationFunctionType

P = 128
B, H, W = 8, 256, 256
HH, HW = H // 2, W // 2
G = 4
BANK = 512
ROWS = 8
CH = ROWS * W
NCH = H // ROWS
SLOTS = 4
NG = NCH // SLOTS
HC = CH // 4
TROWS = 8
TILE = TROWS * HW
NT = HH // TROWS
ACT_TAP = (1, 1)
PE_TAPS = [(0, 0), (0, 1)]
DVE_TAPS = [(0, 2), (1, 0), (1, 2), (2, 0), (2, 1), (2, 2)]
ADDS = len(DVE_TAPS) - 1
DW_LAG = 2
TAP_LAG = 3
SQ_LAG = 4
DVE_PIECES = 3
EPS = 1e-5
TINY = 2.0 ** -30
LEAD = 4

assert HC == BANK and NCH % SLOTS == 0 and TILE == 2 * BANK


def preact_kernel(nc, x, theta_s, w_dw, w_pwT, w_c1T, b_c1, bn1_g, bn1_b, dw_w, dw_b, gn_g, gn_b,
                  pw1_wT, pw1_b, pw2_wT, pw2_b, w_c2T, b_c2, bn2_g, bn2_b, out):
    x1_dram = nc.dram_tensor("x1_dram", (B * NCH, P, CH), F32, kind="Internal").ap()
    y1_dram = nc.dram_tensor("y1_dram", (B * NT, P, TILE), F32, kind="Internal").ap()
    h2_dram = nc.dram_tensor("h2_dram", (B * NT, P, TILE), F32, kind="Internal").ap()

    with ExitStack() as ctx:
        def sb(name, shape, dt=F32):
            return ctx.enter_context(nc.sbuf_tensor(name, shape, dt))

        def sem(name):
            return ctx.enter_context(nc.semaphore(name))

        ident = sb("ident", [P, P])
        group_mean = sb("group_mean", [P, P])
        all_mean = sb("all_mean", [P, P])
        ones = sb("ones", [P, W])
        theta = sb("theta", [P, 2])
        wdw = sb("wdw", [P, 1])
        pwT = sb("pwT", [P, P])
        c1T = sb("c1T", [P, 4, P])
        c1H = sb("c1H", [P, 4, P])
        bc1 = sb("bc1", [P, 1])
        bn1 = sb("bn1", [P, 2])
        taps = sb("taps", [P, 9])
        tap_diag = sb("tap_diag", [P, len(PE_TAPS), P])
        bdw = sb("bdw", [P, 1])
        gn = sb("gn", [P, 2])
        pw1T = sb("pw1T", [P, P])
        bpw1 = sb("bpw1", [P, 1])
        pw2T = sb("pw2T", [P, P])
        bpw2 = sb("bpw2", [P, 1])
        c2T = sb("c2T", [P, 4, P])
        bc2 = sb("bc2", [P, 4])
        bn2 = sb("bn2", [P, 2, 4])

        shift = sb("shift", [P, 8])
        center_y, center_x = shift[:, 0:1], shift[:, 1:2]
        up, left = shift[:, 2:3], shift[:, 3:4]
        down, right = shift[:, 4:5], shift[:, 5:6]
        center_w, inv_center_y = shift[:, 6:7], shift[:, 7:8]

        small = sb("small", [P, 40])
        mom = small[:, 0:2]
        gmom = small[:, 2:4]
        var, std, rstd, tmp = (small[:, k:k + 1] for k in range(4, 8))
        scale0, scale0r, q0, bias0 = (small[:, k:k + 1] for k in range(8, 12))
        pad_u = small[:, 12:13]
        q1, bias1, h_scale, h_bias = (small[:, k:k + 1] for k in range(13, 17))
        ln_scale, ln_shift, bias_pw1, h2_mean = (small[:, k:k + 1] for k in range(17, 21))
        z_mean, z_scale, z_bias = small[:, 21:25], small[:, 25:29], small[:, 29:33]
        pad_x = small[:, 37:38]
        z_tmp, z_std = small[:, 33:37], sb("z_std", [P, 4])
        h2_mean_row = sb("h2_mean_row", [1, 2, P])

        w_center = sb("w_center", [P, P])
        w_right = sb("w_right", [P, P])
        w_c1b = sb("w_c1b", [P, 4, P])
        w_pw1b = sb("w_pw1b", [P, P])
        stats_x = sb("stats_x", [P, NCH * DVE_PIECES * 6])
        sums_x = sb("sums_x", [P, 2, NCH])
        part = sb("part", [P, 2])
        sums_x1 = sb("sums_x1", [P, 2, NCH])
        stats_y1 = sb("stats_y1", [P, B * NCH * 6])
        sums_o = sb("sums_o", [P, 2, NT * 2])
        warm = sb("warm", [P, 1])
        gram = sb("gram", [P, P + 1])
        cov_w = sb("cov_w", [P, 4, P])

        arena = sb("arena", [P, 38700])
        at = [0]

        def cut(n):
            at[0] += n
            assert at[0] <= 38700
            return arena[:, at[0] - n:at[0]]

        ring = cut((SLOTS * ROWS + 2) * W).rearrange("p (r c) -> p r c", c=W)
        u_buf = [cut(ROWS * (W + 2)).rearrange("p (r c) -> p r c", c=W + 2) for _ in range(2)]
        v_buf = [cut(CH) for _ in range(2)]
        x1_buf = [cut(CH) for _ in range(2)]
        ahead = [cut(CH) for _ in range(SLOTS)]
        squares = cut(CH // 2).bitcast(BF16)
        x_copy, x_squares = (cut(BANK // 2).bitcast(BF16) for _ in range(2))
        y1_out = [cut(TILE) for _ in range(2)]
        at[0] = 0
        h_pad = cut((HH + 2) * (HW + 2)).rearrange("p (r c) -> p r c", c=HW + 2)
        o_all = cut(HH * HW).rearrange("p (r c) -> p r c", c=HW)
        y1_in = o_in = [cut(TILE) for _ in range(2)]
        a_buf = [cut(BANK) for _ in range(2)]
        h2_buf = [cut(BANK) for _ in range(2)]
        hT_buf = [cut(4 * (P + 1)).rearrange("p (k c) -> p k c", k=4) for _ in range(2)]
        o_squares = cut(BANK // 2).bitcast(BF16)
        at[0] = (SLOTS * ROWS + 2) * W
        h2_in = [cut(TILE) for _ in range(2)]
        g_buf = [cut(4 * HC).rearrange("p (q n) -> p q n", q=4) for _ in range(2)]
        s_buf = [cut(4 * HC).rearrange("p (n r a c) -> p n r a c", n=2, a=2, c=HW) for _ in range(2)]

        ps = ctx.enter_context(nc.psum_tensor("ps", [P, 8, BANK], F32))
        ps_small = ps[:, 7, :]
        ps_small_x = ps[:, 3, :]

        def banks(k):
            return ps[:, 4 * k:4 * k + 4, :].rearrange("p a n -> p (a n)")

        def slot(s, above=0, below=0):
            return ring[:, 1 + s * ROWS - above:1 + (s + 1) * ROWS + below, :]

        params_in = sem("params_in")
        passed = sem("passed")
        consts_made = sem("consts_made")
        setup_done = sem("setup_done")
        primed = sem("primed")
        dve_step = sem("dve_step")
        mom_ready, gmom_ready = sem("mom_ready"), sem("gmom_ready")
        var_ready, std_ready = sem("var_ready"), sem("std_ready")
        vec_ready, vec_done = sem("vec_ready"), sem("vec_done")
        shift_ready, c1_ready = sem("shift_ready"), sem("c1_ready")
        bn1_ready, ln_ready, bn2_ready = sem("bn1_ready"), sem("ln_ready"), sem("bn2_ready")
        cov_ready, cov_done = sem("cov_ready"), sem("cov_done")
        slot_in = [sem(f"slot_in{s}") for s in range(SLOTS)]
        ahead_in = [sem(f"ahead_in{s}") for s in range(SLOTS)]
        u_up, v_done = sem("u_up"), sem("v_done")
        dw_acc, warmed = sem("dw_acc"), sem("warmed")
        halves_done, out_ready = sem("halves_done"), sem("out_ready")
        y1_loaded = [sem(f"y1_loaded{k}") for k in range(2)]
        h2_loaded = [sem(f"h2_loaded{k}") for k in range(2)]
        xe_loaded = [sem(f"xe_loaded{s}") for s in range(SLOTS)]
        x_counted, x_summed = sem("x_counted"), sem("x_summed")
        x_in_psum, u_done = sem("x_in_psum"), sem("u_done")
        conv_done, x1_ready, sq_done = sem("conv_done"), sem("x1_ready"), sem("sq_done")
        c1_done, y1_ready, y1_counted = sem("c1_done"), sem("y1_ready"), sem("y1_counted")
        h_ready, dw_put, dw_done, dw_taken, o_squared = sem("h_ready"), sem("dw_put"), sem("dw_done"), sem("dw_taken"), sem("o_squared")
        pw1_done, a_ready, pw2_done, h2_ready = sem("pw1_done"), sem("a_ready"), sem("pw2_done"), sem("h2_ready")
        hT_done, hT_ready = sem("hT_done"), sem("hT_ready")
        gram_done, gram_added = sem("gram_done"), sem("gram_added")
        c2_done, g_ready, s_done = sem("c2_done"), sem("g_ready"), sem("s_done")
        x1_stored = [sem(f"x1_stored{k}") for k in range(2)]
        y1_stored = [sem(f"y1_stored{k}") for k in range(2)]
        h2_stored = [sem(f"h2_stored{k}") for k in range(2)]
        out_stored = [sem(f"out_stored{s}") for s in range(SLOTS)]

        def nth(t, back=0):
            return t + (1 + LEAD - back)

        CONSTS = 7
        def adds(b, j):
            return b * (NT * 2 * ADDS) + j * (2 * ADDS)

        PARAMS = [(theta[:, :], theta_s), (wdw[:, :], w_dw), (pwT[:, :], w_pwT), (c1T[:, :, :], w_c1T),
                  (bc1[:, :], b_c1), (bn1[:, 0:1], bn1_g), (bn1[:, 1:2], bn1_b), (taps[:, :], dw_w),
                  (bdw[:, :], dw_b), (gn[:, 0:1], gn_g), (gn[:, 1:2], gn_b), (pw1T[:, :], pw1_wT),
                  (bpw1[:, :], pw1_b), (pw2T[:, :], pw2_wT), (bpw2[:, :], pw2_b), (c2T[:, :, :], w_c2T),
                  (bc2[:, :], b_c2), (bn2[:, 0, :], bn2_g), (bn2[:, 1, :], bn2_b)]

        def wait_alone(eng, value, *sems):
            for s_ in sems:
                eng.wait_ge(s_, value)
            eng.sem_inc(passed, 1)

        block = ctx.enter_context(nc.Block())

        @block.sync
        def _(sp):
            for dst, src in PARAMS:
                sp.dma_start(dst, src).then_inc(params_in, 16)

            def load_x_ahead(b, g, s):
                wait_alone(sp, nth(b * NCH + g * SLOTS + s, SLOTS), x_counted, x_summed)
                sp.dma_start(ahead[s], x[b, :, bass.ds((g * SLOTS + s) * CH, CH)]).then_inc(ahead_in[s], 16)

            def load_ring(b, g, s, first=False, last=False):
                t = b * NCH + g * SLOTS + s
                above, below = int(s == 0 and not first), int(s == SLOTS - 1 and not last)
                wait_alone(sp, nth(t, SLOTS), x_in_psum)
                sp.wait_ge(u_done, nth(t, SLOTS if s == SLOTS - 1 else SLOTS - 1))
                sp.dma_start(slot(s, above, below),
                             x[b, :, bass.ds(((g * SLOTS + s) * ROWS - above) * W, (ROWS + above + below) * W)]
                             .rearrange("p (r c) -> p r c", c=W)).then_inc(slot_in[s], 16)

            def load_group(b, g, following, first=False, last=False):
                for s in range(SLOTS):
                    load_ring(b, g, s, first, last)
                    if following and not first:
                        load_x_ahead(b + 1, g, s)
                if following and first:
                    sp.wait_ge(c1_done, nth(b * NCH, 1))
                    for s in range(SLOTS):
                        load_x_ahead(b + 1, g, s)

            def load_image(b, following):
                load_group(b, 0, following, first=True)
                with sp.Fori(1, NG - 1) as g:
                    load_group(b, g, following)
                load_group(b, NG - 1, following, last=True)
                wait_alone(sp, nth((b + 1 + int(following)) * NCH, 1), x_counted, x_summed)
                with sp.Fori(0, NG) as g:
                    for s in range(SLOTS):
                        wait_alone(sp, nth(b * NCH + g * SLOTS + s, SLOTS), c1_done)
                        sp.wait_ge(x1_stored[s % 2], b * (8 * NCH) + g * (8 * SLOTS) + (s // 2 * 16 + 32))
                        sp.dma_start(ahead[s], x1_dram[b * NCH + g * SLOTS + s]).then_inc(ahead_in[s], 16)

            with sp.Fori(0, NG) as g:
                for s in range(SLOTS):
                    load_x_ahead(0, g, s)
            with sp.Fori(0, B - 1) as b:
                load_image(b, following=True)
            load_image(B - 1, following=False)

            for k in range(2):
                sp.wait_ge(y1_stored[k], 16 * (B * NT // 2) + 16)
            sp.wait_ge(bn1_ready, 1)

            def planes_step(b, i, new, old):
                for k in range(2):
                    j = i * 2 + k
                    if new:
                        sp.wait_ge(h_ready, nth(b * NT + j, 2))
                        sp.dma_start(y1_in[k], y1_dram[b * NT + j]).then_inc(y1_loaded[k], 16)
                    if old:
                        for half in range(2):
                            sp.wait_ge(h2_ready, nth((b - 1) * (2 * NT) + j * 2 + half))
                            sp.dma_start(h2_dram[(b - 1) * NT + j, :, half * BANK:(half + 1) * BANK], h2_buf[half]
                                         ).then_inc(h2_stored[half], 16)

            def planes(b, new=True, old=True):
                with sp.Fori(0, NT // 2) as i:
                    planes_step(b, i, new, old)

            planes(0, old=False)
            with sp.Fori(1, B) as b:
                planes(b)
            planes(B, new=False)

            for k in range(2):
                sp.wait_ge(h2_stored[k], 16 * (B * NT) + 16)
            sp.wait_ge(bn2_ready, 1)

            def load_output_group(g):
                for s in range(SLOTS):
                    if s % 2 == 0:
                        sp.wait_ge(c2_done, nth(g * SLOTS + s, SLOTS - 1))
                        sp.dma_start(h2_in[s // 2], h2_dram[g * 2 + s // 2]).then_inc(h2_loaded[s // 2], 16)
                    if not isinstance(g, int):
                        sp.wait_ge(out_stored[s], g * 16)
                    sp.dma_start(slot(s), x1_dram[g * SLOTS + s].rearrange("p (r c) -> p r c", c=W)
                                 ).then_inc(xe_loaded[s], 16)

            load_output_group(0)
            with sp.Fori(1, B * NG) as g:
                load_output_group(g)
            for s in range(SLOTS):
                sp.wait_ge(out_stored[s], 16 * (B * NG))

        @block.gpsimd
        def _(pool):
            pool.memset(ident[:, :], 0.0).then_inc(consts_made, 1)
            pool.memset(group_mean[:, :], 1.0 / G).then_inc(consts_made, 1)
            pool.memset(all_mean[:, :], 1.0 / P).then_inc(consts_made, 1)
            pool.memset(ones[:, :], 1.0).then_inc(consts_made, 1)
            pool.wait_ge(consts_made, 4)
            pool.affine_select(out=ident[:, :], in_=ident[:, :], compare_op=ALU.not_equal, fill=1.0, base=0,
                               pattern=[[-1, P]], channel_multiplier=1).then_inc(consts_made, 1)
            groups = group_mean[:, :].rearrange("p (g c) -> p g c", c=G)
            pool.affine_select(out=groups, in_=groups, compare_op=ALU.is_ge, fill=0.0, base=0,
                               pattern=[[-G, P // G], [0, G]], channel_multiplier=1).then_inc(consts_made, 1)
            pool.wait_ge(consts_made, 6)
            pool.affine_select(out=groups, in_=groups, compare_op=ALU.is_ge, fill=0.0, base=G - 1,
                               pattern=[[G, P // G], [0, G]], channel_multiplier=-1).then_inc(consts_made, 1)
            with pool.Fori(0, B) as b:
                with pool.Fori(0, NG) as g:
                    for s in range(SLOTS):
                        pool.wait_ge(out_ready, b * NCH + g * SLOTS + (s + 1))
                        pool.dma_start(out[b, :, bass.ds((g * SLOTS + s) * CH, CH)]
                                       .rearrange("p (r c) -> p r c", c=W), slot(s)).then_inc(out_stored[s], 16)

        @block.scalar
        def _(act):
            for stored in x1_stored + y1_stored + h2_stored:
                act.sem_inc(stored, 16)
            for counter in (x_summed, x_in_psum, x1_ready, sq_done, y1_ready, h_ready, dw_put,
                            a_ready, hT_ready, o_squared, g_ready):
                act.sem_inc(counter, LEAD)

            def square_root(n):
                act.wait_ge(var_ready, n)
                nc.scalar.activation(std, var, ACT.Sqrt).then_inc(std_ready, 1)

            def put_x(b, g, s):
                t = b * NCH + g * SLOTS + s
                k = s % 2
                act.wait_ge(slot_in[s], b * (16 * NG) + g * 16 + 16)
                act.wait_ge(x1_ready, nth(t, 2))
                nc.scalar.activation(banks(k), slot(s).rearrange("p r c -> p (r c)"), ACT.Identity,
                                     bias=bias0).then_inc(x_in_psum, 1)

            def take_x1(b, g, s):
                i = g * SLOTS + s
                t = b * NCH + i
                k = s % 2
                act.wait_ge(conv_done, nth(t))
                act.wait_ge(x1_stored[k], b * (8 * NCH) + g * (8 * SLOTS) + (s // 2 * 16 + 16))
                act.wait_ge(sq_done, nth(t, 2))
                nc.scalar.activation(x1_buf[k], banks(k), ACT.Identity,
                                     accum_out=sums_x1[:, 0, bass.ds(i, 1)]).then_inc(x1_ready, 1)
                act.wait_ge(x1_ready, nth(t))
                act.dma_start(x1_dram[t], x1_buf[k]).then_inc(x1_stored[k], 16)
                act.wait_ge(sq_done, nth(t, 1))
                nc.scalar.activation(squares, x1_buf[k], ACT.Square,
                                     accum_out=sums_x1[:, 1, bass.ds(i, 1)]).then_inc(sq_done, 1)

            def sum_x(t, s, i, loaded):
                act.wait_ge(ahead_in[s], loaded)
                wait_alone(act, nth(t, 1), x_summed)
                piece = ahead[s][:, DVE_PIECES * BANK:]
                nc.scalar.activation(x_copy, piece, ACT.Identity, accum_out=sums_x[:, 0, bass.ds(i, 1)])
                nc.scalar.activation(x_squares, piece, ACT.Square,
                                     accum_out=sums_x[:, 1, bass.ds(i, 1)]).then_inc(x_summed, 1)

            def shift_group(b, g, following, first=False):
                for s in range(SLOTS):
                    put_x(b, g, s)
                    if s:
                        take_x1(b, g, s - 1)
                    elif not first:
                        take_x1(b, g - 1, SLOTS - 1)
                    if following:
                        sum_x(b * NCH + g * SLOTS + (NCH + s), s, g * SLOTS + s, b * (32 * NG) + g * 16 + (16 * NG + 16))

            def y1_group(b, g):
                for s in range(SLOTS):
                    t = b * NCH + g * SLOTS + s
                    k = s // 2
                    act.wait_ge(c1_done, nth(t))
                    if s % 2 == 0:
                        act.wait_ge(y1_stored[k], b * (16 * NG) + g * 16 + 16)
                        act.wait_ge(y1_counted, nth(t, SLOTS - 1))
                    nc.scalar.activation(y1_out[k][:, (s % 2) * HC:(s % 2 + 1) * HC], ps[:, s, :],
                                         ACT.Identity, bias=bias1).then_inc(y1_ready, 1)
                    if s % 2 == 1:
                        act.wait_ge(y1_ready, nth(t))
                        act.dma_start(y1_dram[b * NT + g * 2 + k], y1_out[k]).then_inc(y1_stored[k], 16)

            def image(b, following=True):
                act.wait_ge(primed, b + 2)
                shift_group(b, 0, following, first=True)
                with act.Fori(1, NG) as g:
                    shift_group(b, g, following)
                if following:
                    square_root(b * 2 + 2)
                take_x1(b, NG - 1, SLOTS - 1)
                square_root(b * 2 + (3 if following else 2))
                act.wait_ge(c1_ready, b + 1)
                with act.Fori(0, NG) as g:
                    y1_group(b, g)

            with act.Fori(0, NG) as g:
                for s in range(SLOTS):
                    sum_x(g * SLOTS + s, s, g * SLOTS + s, g * 16 + 16)
            square_root(1)
            with act.Fori(0, B - 1) as b:
                image(b)
            image(B - 1, following=False)
            square_root(2 * B + 1)

            act.wait_ge(bn1_ready, 1)

            def square_o(b, j):
                for half in range(2):
                    act.wait_ge(dw_acc, adds(b, j) + ((ADDS - 1) * 2 + half + 1))
                    act.wait_ge(o_squared, nth(b * (2 * NT) + j * 2 + half, 1))
                    nc.scalar.activation(o_squares, o_all[:, bass.ds(j * TROWS + 4 * half, 4), :]
                                         .rearrange("p r c -> p (r c)"), ACT.Square,
                                         accum_out=sums_o[:, 1, bass.ds(j * 2 + half, 1)]).then_inc(o_squared, 1)

            def make_h(b, j, k, count, old):
                if old:
                    act.wait_ge(h2_ready, nth((b - 1) * (2 * NT) + j * 2 + 1))
                act.wait_ge(y1_loaded[k], count * 16 + b * (8 * NT))
                nc.scalar.activation(h_pad[:, bass.ds(j * TROWS + 1, TROWS), 1:HW + 1],
                                     y1_in[k].rearrange("p (r c) -> p r c", c=HW), ACT.Gelu,
                                     bias=h_bias, scale=h_scale).then_inc(h_ready, 1)

            def copy_hT(b, j):
                for half in range(2):
                    act.wait_ge(hT_done, nth(b * (2 * NT) + j * 2 + half))
                    act.wait_ge(gram_done, nth(b * NT + j, 1))
                    nc.scalar.activation(hT_buf[half][:, :, 0:P],
                                         ps[:, 4 + half, :].rearrange("p (k c) -> p k c", k=4),
                                         ACT.Copy).then_inc(hT_ready, 1)

            def put_tap(b, j):
                dy, dx = ACT_TAP
                for half in range(2):
                    act.wait_ge(h_ready, nth(b * NT + j))
                    wait_alone(act, nth(b * (2 * NT) + j * 2 + half, 2), dw_taken)
                    nc.scalar.activation(ps[:, 6 + half, :].rearrange("p (r c) -> p r c", c=HW),
                                         h_pad[:, bass.ds(j * TROWS + (4 * half + dy), 4), dx:dx + HW],
                                         ACT.Copy, scale=taps[:, 3 * dy + dx:3 * dy + dx + 1]).then_inc(dw_put, 1)

            def planes_step(b, i, new, old):
                for k in range(2):
                    j = i * 2 + k
                    first = isinstance(j, int) and j == 0
                    n = (b - 1) * (2 * NT) + j * 2
                    if new and not first:
                        make_h(b, j - 1, 1 - k, i + k, old)
                    if old:
                        for half in range(2):
                            act.wait_ge(pw1_done, nth(n + half))
                            act.wait_ge(pw2_done, nth(n + half, 2))
                            nc.scalar.activation(a_buf[half], ps[:, half, :], ACT.Gelu,
                                                 bias=bias_pw1).then_inc(a_ready, 1)
                    if old and not first:
                        copy_hT(b - 1, j - 1)
                    if new and not (isinstance(j, int) and j < SQ_LAG):
                        square_o(b, j - SQ_LAG)
                    if new and not first:
                        put_tap(b, j - 1)

            def warm_gelu(n):
                act.wait_ge(warmed, n)
                nc.scalar.activation(warm[:, :], ones[:, 0:1], ACT.Gelu).then_inc(warmed, 1)

            def planes(b, new=True, old=True):
                warm_gelu(b)
                if old:
                    act.wait_ge(ln_ready, b)
                if new:
                    act.wait_ge(primed, b + (B + 2))
                for i in range(2):
                    planes_step(b, i, new, old)
                with act.Fori(2, NT // 2) as i:
                    planes_step(b, i, new, old)
                if new:
                    make_h(b, NT - 1, 1, NT // 2, old)
                if old:
                    copy_hT(b - 1, NT - 1)
                if new:
                    put_tap(b, NT - 1)
                    for j in range(NT - SQ_LAG, NT):
                        square_o(b, j)
                    square_root(b + (2 * B + 2))

            planes(0, old=False)
            with act.Fori(1, B) as b:
                planes(b)
            planes(B, new=False)

            act.wait_ge(var_ready, 3 * B + 2)
            nc.scalar.activation(z_std[:, :], z_tmp, ACT.Sqrt).then_inc(std_ready, 1)
            warm_gelu(B + 1)
            act.wait_ge(bn2_ready, 1)
            with act.Fori(0, B * NCH // 2) as i:
                for k in range(2):
                    act.wait_ge(c2_done, nth(i * 2 + k))
                    act.wait_ge(s_done, nth(i * 2 + k, 2))
                    for q in range(4):
                        last = nc.scalar.activation(g_buf[k][:, q, :], ps[:, 4 * k + q, :], ACT.Gelu,
                                                    bias=z_bias[:, q:q + 1], scale=z_scale[:, q:q + 1])
                    last.then_inc(g_ready, 1)

        @block.tensor
        def _(pe):
            mm = nc.tensor.matmul
            for counter in (conv_done, c1_done, dw_done, pw1_done, pw2_done, hT_done, gram_done, c2_done):
                pe.sem_inc(counter, LEAD)

            def channel_means(n, weights, ps_small=ps_small):
                pe.wait_ge(mom_ready, n)
                mm(ps_small[:, 0:2], weights[:, :], mom, start=True, stop=True).then_inc(gmom_ready, 1)

            def vector_product(n, weights, vec, ps_small=ps_small):
                pe.wait_ge(vec_ready, n)
                mm(ps_small[:, 4:5], weights, vec, start=True, stop=True).then_inc(vec_done, 1)

            def shift_group(b, g):
                for s in range(SLOTS):
                    t = b * NCH + g * SLOTS + s
                    k = s % 2
                    pe.wait_ge(u_done, nth(t))
                    pe.wait_ge(x_in_psum, nth(t))
                    for r in range(4):
                        mm(ps[:, 4 * k + r, :], w_right[:, :], u_buf[k][:, 2 * r:2 * r + 2, 2:W + 2],
                           start=False, stop=False, skip_group_check=True)
                    pe.wait_ge(v_done, t + 1)
                    for r in range(4):
                        last = mm(ps[:, 4 * k + r, :], w_center[:, :], v_buf[k][:, r * BANK:(r + 1) * BANK],
                                  start=False, stop=True, skip_group_check=True)
                    last.then_inc(conv_done, 1)

            def c1_group(b, g, last_image):
                for s in range(SLOTS):
                    t = b * NCH + g * SLOTS + s
                    pe.wait_ge(ahead_in[s], b * (32 * NG) + g * 16 + ((16 if last_image else 32) * NG + 16))
                    pe.wait_ge(y1_ready, nth(t, SLOTS))
                    cells = ahead[s].rearrange("p (r a c e) -> p a e r c", a=2, c=HW, e=2)
                    for q in range(4):
                        last = mm(ps[:, s, :], w_c1b[:, q, :], cells[:, q // 2, q % 2, :, :],
                                  start=(q == 0), stop=(q == 3))
                    last.then_inc(c1_done, 1)

            def prime(bank):
                return mm(ps[:, bank, :], ident[:, :], c2T[:, :, :], start=True, stop=True)

            def image(b, last_image=False):
                pe.wait_ge(shift_ready, b + 1)
                prime(7).then_inc(primed, 1)
                pe.wait_ge(primed, b + 2)
                shift_group(b, 0)
                with pe.Fori(1, NG) as g:
                    shift_group(b, g)
                if not last_image:
                    pe.wait_ge(x1_ready, nth(b * NCH, 2 - NCH))
                    prepare_x(b * 2 + 2)
                x1_step = b * 2 + (2 if last_image else 3)
                channel_means(x1_step, group_mean)
                vector_product(x1_step, c1T[:, 0, :], q1)
                wait_alone(pe, b + 1, c1_ready)
                with pe.Fori(0, NG) as g:
                    c1_group(b, g, last_image)

            def prepare_x(n):
                channel_means(n, group_mean, ps_small_x)
                vector_product(n, pwT[:, :], q0, ps_small_x)

            pe.wait_ge(setup_done, 1)
            prepare_x(1)
            pe.wait_ge(shift_ready, 1)
            for bank in range(7):
                last = prime(bank)
            last.then_inc(primed, 1)
            with pe.Fori(0, B - 1) as b:
                image(b)
            image(B - 1, last_image=True)

            def first_conv(b, j, back):
                n = b * (2 * NT) + j * 2
                pe.wait_ge(gram_added, nth(b * NT + j, back))
                for half in range(2):
                    pe.wait_ge(a_ready, nth(n + half, 2))
                    mm(ps[:, half, :], w_pw1b[:, :], o_all[:, bass.ds(j * TROWS + 4 * half, 4), :],
                       start=True, stop=True).then_inc(pw1_done, 1)

            def second_conv(b, j):
                n = b * (2 * NT) + j * 2
                for half in range(2):
                    pe.wait_ge(a_ready, nth(n + half))
                    pe.wait_ge(h2_ready, nth(n + half, 2))
                    mm(ps[:, 2 + half, :], pw2T[:, :], a_buf[half], start=True, stop=True).then_inc(pw2_done, 1)

            def turn_h2(b, j):
                n = b * (2 * NT) + j * 2
                for half in range(2):
                    pe.wait_ge(h2_ready, nth(n + half))
                    pe.wait_ge(hT_ready, nth(n + half, 2))
                    for c in range(4):
                        last = nc.tensor.transpose(ps[:, 4 + half, c * P:(c + 1) * P],
                                                   h2_buf[half][:, c * P:(c + 1) * P], ident[:, :])
                    last.then_inc(hT_done, 1)

            def gram_tile(b, j):
                n = b * (2 * NT) + j * 2
                pe.wait_ge(gram_added, nth(b * NT + j, 1))
                for half in range(2):
                    pe.wait_ge(hT_ready, nth(n + half))
                    for c in range(4):
                        last = mm(ps[:, 0, 0:P + 1], hT_buf[half][:, c, 0:P], hT_buf[half][:, c, :],
                                  start=(half == 0 and c == 0), stop=(half == 1 and c == 3))
                last.then_inc(gram_done, 1)

            def dw_half(b, j, half, last_tile=False):
                below = any(dy == 2 for dy, _ in PE_TAPS) and not last_tile
                pe.wait_ge(h_ready, nth(b * NT + j, -int(below)))
                pe.wait_ge(dw_put, nth(b * (2 * NT) + j * 2 + half))
                for n, (dy, dx) in enumerate(PE_TAPS):
                    last = mm(ps[:, 6 + half, :], tap_diag[:, n, :],
                              h_pad[:, bass.ds(j * TROWS + (4 * half + dy), 4), dx:dx + HW],
                              start=False, stop=(n == len(PE_TAPS) - 1), skip_group_check=True)
                last.then_inc(dw_done, 1)

            def planes_step(b, j, new, old):
                early = isinstance(j, int)
                before = old and not (early and j == 0)
                if old:
                    first_conv(b - 1, j, back=1 if early and j == 0 else 2)
                if before:
                    turn_h2(b - 1, j - 1)
                if new and not early:
                    dw_half(b, j - DW_LAG, 0)
                if before:
                    gram_tile(b - 1, j - 1)
                if new and not early:
                    dw_half(b, j - DW_LAG, 1)
                if old:
                    second_conv(b - 1, j)

            def planes(b, new=True, old=True):
                if old:
                    pe.wait_ge(ln_ready, b)
                if new:
                    prime(7).then_inc(primed, 1)
                for j in range(DW_LAG):
                    planes_step(b, j, new, old)
                with pe.Fori(DW_LAG // 2, NT // 2) as i:
                    for k in range(2):
                        planes_step(b, i * 2 + k, new, old)
                if old:
                    turn_h2(b - 1, NT - 1)
                    gram_tile(b - 1, NT - 1)
                if new:
                    for j in range(NT - DW_LAG, NT):
                        for half in range(2):
                            dw_half(b, j, half, last_tile=(j == NT - 1))
                    channel_means(b + (2 * B + 1), all_mean)
                    vector_product(b + (2 * B + 1), pw1T[:, :], ln_shift)

            pe.wait_ge(bn1_ready, 1)
            planes(0, old=False)
            with pe.Fori(1, B) as b:
                planes(b)
            planes(B, new=False)

            pe.wait_ge(cov_ready, 1)
            mm(ps[0:1, 0, 0:P], h2_mean, ident[:, :], start=True, stop=True).then_inc(cov_done, 1)
            pe.wait_ge(cov_ready, 2)
            mm(ps[:, 1, 0:P], h2_mean_row[:, 0, :], h2_mean_row[:, 1, :], start=True, stop=True).then_inc(cov_done, 1)
            pe.wait_ge(cov_ready, 3)
            mm(ps[:, 2, :], gram[:, 0:P], c2T[:, :, :], start=True, stop=True)
            for q in range(4):
                last = mm(ps[:, 3, q:q + 1], c2T[:, q, :], h2_mean, start=True, stop=True)
            last.then_inc(cov_done, 1)
            pe.wait_ge(cov_ready, 4)
            for q in range(4):
                last = mm(ps[:, 4, q:q + 1], cov_w[:, q, :], ones[:, 0:1], start=True, stop=True)
            last.then_inc(cov_done, 1)

            pe.wait_ge(bn2_ready, 1)
            with pe.Fori(0, B * NG) as g:
                for s in range(SLOTS):
                    k = s % 2
                    if k == 0:
                        pe.wait_ge(h2_loaded[s // 2], g * 16 + 16)
                    pe.wait_ge(g_ready, nth(g * SLOTS + s, 2))
                    for q in range(4):
                        last = mm(ps[:, 4 * k + q, :], c2T[:, q, :], h2_in[s // 2][:, k * HC:(k + 1) * HC],
                                  start=True, stop=True)
                    last.then_inc(c2_done, 1)

        @block.vector
        def _(dve):
            stt, ts, tt = nc.vector.scalar_tensor_tensor, nc.vector.tensor_scalar, nc.vector.tensor_tensor
            for counter in (x_counted, u_done, y1_counted, dw_taken, h2_ready, gram_added, s_done):
                dve.sem_inc(counter, LEAD)

            steps = [0, 0]

            def start_steps(base):
                steps[0], steps[1] = base, 0

            def done(ins):
                steps[1] += 1
                ins.then_inc(dve_step, 1)
                dve.wait_ge(dve_step, steps[0] + steps[1])

            def refine(r, s, v):
                done(nc.vector.reciprocal(r, s))
                done(tt(s, r, r, ALU.mult))
                done(tt(s, s, v, ALU.mult))
                done(ts(s, s, -0.5, 1.5, ALU.mult, ALU.add))
                done(tt(r, r, s, ALU.mult))

            def normaliser(n, nth_root, ps_small=ps_small):
                dve.wait_ge(gmom_ready, n)
                done(nc.vector.tensor_copy(gmom, ps_small[:, 0:2]))
                done(stt(out=tmp, in0=gmom[:, 0:1], scalar=gmom[:, 0:1], in1=gmom[:, 1:2],
                         op0=ALU.mult, op1=ALU.subtract))
                done(ts(tmp, tmp, 0.0, -1.0, ALU.min, ALU.mult))
                root(nth_root)

            def root(n):
                ts(var, tmp, EPS, None, ALU.add).then_inc(var_ready, 1)
                dve.wait_ge(std_ready, n)
                refine(rstd, std, var)

            dve.wait_ge(params_in, 16 * len(PARAMS))
            dve.wait_ge(consts_made, CONSTS)
            start_steps(0)
            for axis, center, inverse, before, after in ((0, center_y, inv_center_y, up, down),
                                                         (1, center_x, center_w, left, right)):
                th = theta[:, axis:axis + 1]
                done(ts(tmp, th, -1.0, None, ALU.mult))
                done(tt(center, th, tmp, ALU.max))
                done(ts(center, center, -1.0, 1.0, ALU.mult, ALU.add))
                done(ts(center, center, TINY, None, ALU.max))
                done(nc.vector.reciprocal(inverse, center))
                done(ts(before, th, 0.0, None, ALU.max))
                done(tt(before, before, inverse, ALU.mult))
                done(ts(after, tmp, 0.0, None, ALU.max))
                done(tt(after, after, inverse, ALU.mult))
            done(tt(center_w, center_y, center_x, ALU.mult))
            done(tt(center_w, center_w, wdw[:, :], ALU.mult))
            ll, lh, hl, hh = (c1T[:, q, :] for q in range(4))
            tt(cov_w[:, 0, :], ll, lh, ALU.add)
            tt(cov_w[:, 1, :], ll, lh, ALU.subtract)
            tt(cov_w[:, 2, :], hl, hh, ALU.add)
            done(tt(cov_w[:, 3, :], hl, hh, ALU.subtract))
            tt(c1H[:, 0, :], cov_w[:, 0, :], cov_w[:, 2, :], ALU.add)
            tt(c1H[:, 1, :], cov_w[:, 0, :], cov_w[:, 2, :], ALU.subtract)
            tt(c1H[:, 2, :], cov_w[:, 1, :], cov_w[:, 3, :], ALU.add)
            done(tt(c1H[:, 3, :], cov_w[:, 1, :], cov_w[:, 3, :], ALU.subtract))
            done(ts(c1H[:, :, :], c1H[:, :, :], 0.5, None, ALU.mult))
            for n, (dy, dx) in enumerate(PE_TAPS):
                ts(tap_diag[:, n, :], ident[:, :], taps[:, 3 * dy + dx:3 * dy + dx + 1], None, ALU.mult)
            nc.vector.memset(gram[:, :], 0.0).then_inc(setup_done, 1)
            dve.wait_ge(setup_done, 1)
            SETUP_STEPS = 23
            assert steps[1] == SETUP_STEPS

            def count_x(b, g, s, pieces=range(DVE_PIECES)):
                seen = g * 16 + 16 if isinstance(b, int) else (b - 1) * (32 * NG) + g * 16 + (16 * NG + 16)
                if 0 in pieces:
                    dve.wait_ge(ahead_in[s], seen)
                for r in pieces:
                    last = nc.vector.bn_stats(stats_x[:, bass.ds((g * SLOTS + s) * (6 * DVE_PIECES) + 6 * r, 6)],
                                              ahead[s][:, r * BANK:(r + 1) * BANK])
                if DVE_PIECES - 1 in pieces:
                    last.then_inc(x_counted, 1)

            def shift_rows(b, g, s, following):
                t = b * NCH + g * SLOTS + s
                k = s % 2
                for near in range(s, min(s + 2, SLOTS)):
                    dve.wait_ge(slot_in[near], b * (16 * NG) + g * 16 + 16)
                dve.wait_ge(conv_done, nth(t, 2))
                u = u_buf[k][:, :, 1:W + 1]
                stt(out=u, in0=ring[:, s * ROWS:(s + 1) * ROWS, :], scalar=up, in1=slot(s),
                    op0=ALU.mult, op1=ALU.add).then_inc(u_up, 1)
                if following:
                    count_x(b + 1, g, s, range(0, 2))
                dve.wait_ge(u_up, t + 1)
                stt(out=u, in0=ring[:, s * ROWS + 2:(s + 1) * ROWS + 2, :], scalar=down, in1=u,
                    op0=ALU.mult, op1=ALU.add).then_inc(u_done, 1)
                if following:
                    count_x(b + 1, g, s, range(2, DVE_PIECES))
                dve.wait_ge(u_done, nth(t))
                stt(out=v_buf[k].rearrange("p (r c) -> p r c", c=W), in0=u_buf[k][:, :, 0:W], scalar=left, in1=u,
                    op0=ALU.mult, op1=ALU.add).then_inc(v_done, 1)

            def shift_group(b, g, following):
                for s in range(SLOTS):
                    shift_rows(b, g, s, following)

            def pad_row(row):
                return ts(ring[:, row, :], ones[:, :], pad_x, None, ALU.mult)

            IMAGE_STEPS = 27

            def prepare_x(b, n):
                wait_alone(dve, nth(b * NCH, 1 - NCH), x_counted, x_summed)
                nc.vector.tensor_reduce(part[:, :], sums_x[:, :, :], mybir.AxisListType.X, ALU.add)
                done(nc.vector.bn_aggr(mom, stats_x[:, :]))
                ts(part[:, :], part[:, :], 1.0 / (H * W), None, ALU.mult)
                done(stt(out=mom[:, 1:2], in0=mom[:, 0:1], scalar=mom[:, 0:1], in1=mom[:, 1:2],
                         op0=ALU.mult, op1=ALU.add))
                stt(out=mom, in0=mom, scalar=DVE_PIECES / 4, in1=part[:, :],
                    op0=ALU.mult, op1=ALU.add).then_inc(mom_ready, 1)
                normaliser(n, n, ps_small_x)
                ts(pad_x, gmom[:, 0:1], 1.0, None, ALU.mult)
                done(tt(scale0, center_w, rstd, ALU.mult))
                done(tt(scale0r, scale0, right, ALU.mult))
                done(tt(q0, wdw[:, :], rstd, ALU.mult))
                tt(q0, q0, gmom[:, 0:1], ALU.mult).then_inc(vec_ready, 1)
                ts(w_center[:, :], pwT[:, :], scale0, None, ALU.mult)
                ts(w_right[:, :], pwT[:, :], scale0r, None, ALU.mult)
                done(tt(pad_u, gmom[:, 0:1], inv_center_y, ALU.mult))
                for k in range(2):
                    for col in (0, W + 1):
                        ts(u_buf[k][:, :, col], ones[:, 0:ROWS], pad_u, None, ALU.mult)
                done(pad_row(0))
                dve.wait_ge(vec_done, n)
                done(ts(bias0, ps_small_x[:, 4:5], -1.0, None, ALU.mult))
                ts(tmp, bias0, 1.0, None, ALU.mult).then_inc(shift_ready, 1)

            def image(b, following=True):
                start_steps(b * IMAGE_STEPS + (SETUP_STEPS + X_STEPS))
                wait_alone(dve, b + 1, shift_ready)
                with dve.Fori(0, NG - 1) as g:
                    shift_group(b, g, following)
                done(pad_row(SLOTS * ROWS + 1))
                shift_group(b, NG - 1, following)

                if following:
                    prepare_x(b + 1, b * 2 + 2)
                n = b * 2 + (3 if following else 2)

                dve.wait_ge(x1_ready, nth(b * NCH, 1 - NCH))
                dve.wait_ge(sq_done, nth(b * NCH, 1 - NCH))
                done(nc.vector.tensor_reduce(mom, sums_x1[:, :, :], mybir.AxisListType.X, ALU.add))
                ts(mom, mom, 1.0 / (H * W), None, ALU.mult).then_inc(mom_ready, 1)
                normaliser(n, n)
                tt(q1, rstd, gmom[:, 0:1], ALU.mult).then_inc(vec_ready, 1)
                done(ts(w_c1b[:, :, :], c1H[:, :, :], rstd, None, ALU.mult))
                dve.wait_ge(vec_done, n)
                stt(out=bias1, in0=ps_small[:, 4:5], scalar=-2.0, in1=bc1[:, :],
                    op0=ALU.mult, op1=ALU.add).then_inc(c1_ready, 1)

                with dve.Fori(0, NG) as g:
                    for s in range(SLOTS):
                        t = b * NCH + g * SLOTS + s
                        dve.wait_ge(y1_ready, nth(t))
                        nc.vector.bn_stats(stats_y1[:, bass.ds(t * 6, 6)],
                                           y1_out[s // 2][:, (s % 2) * HC:(s % 2 + 1) * HC]
                                           ).then_inc(y1_counted, 1)

            with dve.Fori(0, NG) as g:
                for s in range(SLOTS):
                    count_x(0, g, s)
            start_steps(SETUP_STEPS)
            prepare_x(0, 1)
            X_STEPS = steps[1]
            with dve.Fori(0, B - 1) as b:
                image(b)
            assert steps[1] == IMAGE_STEPS
            image(B - 1, following=False)
            assert steps[1] == IMAGE_STEPS - X_STEPS

            start_steps(B * IMAGE_STEPS + SETUP_STEPS)
            dve.wait_ge(y1_counted, nth(B * NCH, 1))
            done(nc.vector.bn_aggr(mom, stats_y1[:, :]))
            done(ts(tmp, mom[:, 1:2], 1.0, None, ALU.mult))
            root(2 * B + 1)
            done(tt(h_scale, bn1[:, 0:1], rstd, ALU.mult))
            done(tt(tmp, mom[:, 0:1], h_scale, ALU.mult))
            tt(h_bias, bn1[:, 1:2], tmp, ALU.subtract)
            for k in range(2):
                dve.wait_ge(y1_stored[k], 16 * (B * NT // 2) + 16)
            for edge in (0, HH + 1):
                nc.vector.memset(h_pad[:, edge, :], 0.0)
            for edge in (0, HW + 1):
                nc.vector.memset(h_pad[:, 1:HH + 1, edge], 0.0)
            for k in range(2):
                last = nc.vector.memset(hT_buf[k][:, :, P], 1.0)
            last.then_inc(bn1_ready, 1)
            dve.wait_ge(bn1_ready, 1)
            MIDDLE = B * IMAGE_STEPS + SETUP_STEPS + steps[1]

            def make_h2(b, j):
                for half in range(2):
                    n = b * (2 * NT) + j * 2 + half
                    dve.wait_ge(pw2_done, nth(n))
                    dve.wait_ge(h2_stored[half], b * (16 * NT) + j * 16 + 16)
                    dve.wait_ge(hT_done, nth(n, 2))
                    stt(out=h2_buf[half].rearrange("p (r c) -> p r c", c=HW),
                        in0=ps[:, 2 + half, :].rearrange("p (r c) -> p r c", c=HW), scalar=bpw2[:, :],
                        in1=h_pad[:, bass.ds(j * TROWS + (4 * half + 1), 4), 1:HW + 1],
                        op0=ALU.add, op1=ALU.add).then_inc(h2_ready, 1)

            def tap(i, j, half):
                dy, dx = DVE_TAPS[i]
                return (o_all[:, bass.ds(j * TROWS + 4 * half, 4), :],
                        h_pad[:, bass.ds(j * TROWS + (4 * half + dy), 4), dx:dx + HW],
                        taps[:, 3 * dy + dx:3 * dy + dx + 1])

            def take_taps(b, j, last_tile=False):
                dve.wait_ge(h_ready, nth(b * NT + j, 0 if last_tile else -1))
                for half in range(2):
                    o, h, w = tap(0, j, half)
                    dve.wait_ge(dw_done, nth(b * (2 * NT) + j * 2 + half))
                    stt(out=o, in0=h, scalar=w, in1=ps[:, 6 + half, :].rearrange("p (r c) -> p r c", c=HW),
                        op0=ALU.mult, op1=ALU.add).then_inc(dw_taken, 1)

            def add_taps(b, j, first, end):
                for i in range(first, end):
                    for half in range(2):
                        o, h, w = tap(i, j, half)
                        if i == 1:
                            dve.wait_ge(dw_taken, nth(b * (2 * NT) + j * 2 + half))
                        else:
                            dve.wait_ge(dw_acc, adds(b, j) + (2 * (i - 2) + half + 1))
                        total = sums_o[:, 0, bass.ds(j * 2 + half, 1)] if i == ADDS else None
                        stt(out=o, in0=h, scalar=w, in1=o, op0=ALU.mult, op1=ALU.add,
                            accum_out=total).then_inc(dw_acc, 1)

            def add_gram(b, j):
                dve.wait_ge(gram_done, nth(b * NT + j))
                dve.wait_ge(gram_added, nth(b * NT + j, 1))
                tt(gram[:, :], gram[:, :], ps[:, 0, 0:P + 1], ALU.add).then_inc(gram_added, 1)

            def planes_step(b, j, new, old):
                early = isinstance(j, int)
                if new and not (early and j < TAP_LAG):
                    add_taps(b, j - TAP_LAG, 1, ADDS + 1)
                if old and not (early and j == 0):
                    add_gram(b - 1, j - 1)
                if new and not (early and j < DW_LAG):
                    take_taps(b, j - DW_LAG)
                if old:
                    make_h2(b - 1, j)

            PLANE_STEPS = 15

            def planes(b, new=True, old=True):
                for j in range(TAP_LAG + 1):
                    planes_step(b, j, new, old)
                with dve.Fori((TAP_LAG + 1) // 2, NT // 2) as i:
                    for k in range(2):
                        planes_step(b, i * 2 + k, new, old)
                if old:
                    add_gram(b - 1, NT - 1)
                if not new:
                    return
                for j in range(NT - TAP_LAG, NT):
                    if j >= NT - DW_LAG:
                        take_taps(b, j, last_tile=(j == NT - 1))
                    add_taps(b, j, 1, ADDS + 1)
                start_steps(b * PLANE_STEPS + MIDDLE)
                dve.wait_ge(dw_acc, adds(b, NT))
                dve.wait_ge(o_squared, nth(b * (2 * NT), 1 - 2 * NT))
                done(nc.vector.tensor_reduce(mom, sums_o[:, :, :], mybir.AxisListType.X, ALU.add))
                done(ts(mom, mom, 1.0 / (HH * HW), None, ALU.mult))
                done(stt(out=tmp, in0=mom[:, 0:1], scalar=mom[:, 0:1], in1=mom[:, 1:2],
                         op0=ALU.mult, op1=ALU.subtract))
                done(tt(mom[:, 0:1], mom[:, 0:1], bdw[:, :], ALU.add))
                stt(out=mom[:, 1:2], in0=mom[:, 0:1], scalar=mom[:, 0:1], in1=tmp,
                    op0=ALU.mult, op1=ALU.subtract).then_inc(mom_ready, 1)
                normaliser(b + (2 * B + 1), b + (2 * B + 2))
                done(tt(ln_scale, rstd, gn[:, 0:1], ALU.mult))
                done(stt(out=ln_shift, in0=bdw[:, :], scalar=gmom[:, 0:1], in1=ln_scale,
                         op0=ALU.subtract, op1=ALU.mult))
                tt(ln_shift, ln_shift, gn[:, 1:2], ALU.add).then_inc(vec_ready, 1)
                done(ts(w_pw1b[:, :], pw1T[:, :], ln_scale, None, ALU.mult))
                dve.wait_ge(vec_done, b + (2 * B + 1))
                tt(bias_pw1, ps_small[:, 4:5], bpw1[:, :], ALU.add).then_inc(ln_ready, 1)


            planes(0, old=False)
            with dve.Fori(1, B) as b:
                planes(b)
            planes(B, new=False)
            assert steps[1] == PLANE_STEPS

            start_steps(MIDDLE + B * PLANE_STEPS)
            count = float(B * HH * HW)
            dve.wait_ge(gram_added, nth(B * NT, 1))
            ts(h2_mean, gram[:, P:P + 1], 1.0 / count, None, ALU.mult).then_inc(cov_ready, 1)
            dve.wait_ge(cov_done, 1)
            ts(h2_mean_row[:, 0, :], ps[0:1, 0, 0:P], -1.0, None, ALU.mult)
            nc.vector.tensor_copy(h2_mean_row[:, 1, :], ps[0:1, 0, 0:P]).then_inc(cov_ready, 1)
            dve.wait_ge(cov_done, 2)
            stt(out=gram[:, 0:P], in0=gram[:, 0:P], scalar=1.0 / count, in1=ps[:, 1, 0:P],
                op0=ALU.mult, op1=ALU.add).then_inc(cov_ready, 1)
            dve.wait_ge(cov_done, 3)
            tt(z_mean, ps[:, 3, 0:4], bc2[:, :], ALU.add)
            tt(cov_w[:, :, :], ps[:, 2, :].rearrange("p (q n) -> p q n", q=4), c2T[:, :, :],
               ALU.mult).then_inc(cov_ready, 1)
            dve.wait_ge(cov_done, 4)
            ts(z_tmp, ps[:, 4, 0:4], 0.0, EPS, ALU.max, ALU.add).then_inc(var_ready, 1)
            dve.wait_ge(std_ready, 3 * B + 2)
            refine(z_scale, z_std[:, :], z_tmp)
            done(tt(z_scale, z_scale, bn2[:, 0, :], ALU.mult))
            done(tt(z_bias, bc2[:, :], z_mean, ALU.subtract))
            done(tt(z_bias, z_bias, z_scale, ALU.mult))
            for k in range(2):
                dve.wait_ge(h2_stored[k], 16 * (B * NT) + 16)
            tt(z_bias, z_bias, bn2[:, 1, :], ALU.add).then_inc(bn2_ready, 1)

            with dve.Fori(0, B * NG) as g:
                for s in range(SLOTS):
                    t = g * SLOTS + s
                    k = s % 2
                    even, odd = (g_buf[k][:, q::2, :].rearrange("p q (r c) -> p q r c", c=HW) for q in range(2))
                    dve.wait_ge(g_ready, nth(t))
                    tt(s_buf[k][:, :, :, 0, :], even, odd, ALU.add)
                    tt(s_buf[k][:, :, :, 1, :], even, odd, ALU.subtract).then_inc(s_done, 1)
                    dve.wait_ge(s_done, nth(t))
                    dve.wait_ge(xe_loaded[s], g * 16 + 16)
                    pairs = slot(s).rearrange("p r (c e) -> p (r c) e", e=2)
                    low, high = (s_buf[k][:, n].rearrange("p r a c -> p (r a c)") for n in range(2))
                    stt(out=pairs, in0=low.rearrange("p (n e) -> p n e", e=1).broadcast_to([P, CH // 2, 2]),
                        scalar=0.5, in1=pairs, op0=ALU.mult, op1=ALU.add).then_inc(halves_done, 1)
                    dve.wait_ge(halves_done, t + 1)
                    for e in range(2):
                        last = stt(out=pairs[:, :, e], in0=high, scalar=0.5 - e, in1=pairs[:, :, e],
                                   op0=ALU.mult, op1=ALU.add)
                    last.then_inc(out_ready, 1)


def kernel(**inputs):
    import numpy as np
    import concourse.bacc as bacc
    from concourse.bass_utils import run_bass_kernel_spmd

    def arr(name):
        return np.asarray(inputs[name])

    def column(name):
        return arr(name).reshape(P, 1)

    L1 = "L1_conv_"
    laid = {
        "x": arr("x").reshape(B, P, H * W),
        "theta_s": arr("L0_conv_theta_s"),
        "w_dw": column("L0_conv_w_dw"),
        "w_pwT": arr("L0_conv_w_pw").T,
        "w_c1T": arr(L1 + "w_c1").reshape(P, 4, P).transpose(2, 1, 0),
        "b_c1": column(L1 + "b_c1"),
        "bn1_g": column(L1 + "bn1_g"),
        "bn1_b": column(L1 + "bn1_b"),
        "dw_w": arr(L1 + "dw_w").reshape(P, 9),
        "dw_b": column(L1 + "dw_b"),
        "gn_g": column(L1 + "gn_g"),
        "gn_b": column(L1 + "gn_b"),
        "pw1_wT": arr(L1 + "pw1_w").T,
        "pw1_b": column(L1 + "pw1_b"),
        "pw2_wT": arr(L1 + "pw2_w").T,
        "pw2_b": column(L1 + "pw2_b"),
        "w_c2T": arr(L1 + "w_c2").reshape(4, P, P).transpose(2, 0, 1),
        "b_c2": arr(L1 + "b_c2").reshape(4, P).T,
        "bn2_g": arr(L1 + "bn2_g").reshape(4, P).T,
        "bn2_b": arr(L1 + "bn2_b").reshape(4, P).T,
    }
    nc = bacc.Bacc("TRN2", target_bir_lowering=False, num_devices=1)
    feed, args = {}, {}
    for name, a in laid.items():
        a = np.ascontiguousarray(a)
        feed["in_" + name] = a
        args[name] = nc.dram_tensor("in_" + name, a.shape, mybir.dt.from_np(a.dtype), kind="ExternalInput").ap()
    args["out"] = nc.dram_tensor("out_x", (B, P, H * W), F32, kind="ExternalOutput").ap()
    preact_kernel(nc, **args)
    r = run_bass_kernel_spmd(nc, [feed], core_ids=[0])
    return r.results[0]["out_x"].reshape(B, P, H, W)
```
